# Optimizing a Trainium2 kernel written in Bass

```python
import numpy as np
import jax
import jax.numpy as jnp

def _softmax(x, axis=-1):
    return jax.nn.softmax(x, axis=axis)

def _gelu(x):
    return jax.nn.gelu(x, approximate=True)

def _silu(x):
    return jax.nn.silu(x)

def _sigmoid(x):
    return jax.nn.sigmoid(x)

def _layernorm(x, axis=-1, eps=1e-05):
    m = jnp.mean(x, axis=axis, keepdims=True)
    v = jnp.var(x, axis=axis, keepdims=True)
    return (x - m) / jnp.sqrt(v + eps)

def _scatter_add(tgt, idx, src, axis=0):
    return tgt.at[idx].add(src)

def _segment_sum(src, seg, n):
    return jax.ops.segment_sum(src, seg, n)
kernel_name = 'mk_gps_d1_gnn_r8_279129'

def setup_inputs(seed: int=0):
    np.random.seed(seed)
    _w = jnp.asarray

    def _rec_inputs():
        import jax
        import jax.numpy as jnp
        _gk = jax.random.key(seed)
        x = -0.0002117 + 1 * jax.random.normal(jax.random.fold_in(_gk, 1), (6250, 256), jnp.float32)
        src = jax.random.randint(jax.random.fold_in(_gk, 2), (200000,), 0, 6250, jnp.int32)
        dst = jnp.minimum((6250 * jax.random.uniform(jax.random.fold_in(_gk, 3), (200000,)) ** 2.0).astype(jnp.int32), 49999)
        _o = jnp.argsort(dst, stable=True)
        src = src[_o]
        dst = dst[_o]
        return (x, src, dst)
    x, src, dst = _rec_inputs()

    def _L0_gnn_setup():
        import jax, jax.numpy as jnp
        import numpy as np
        N_NODES = 12500
        N_EDGES = 37500
        D_IN = 256
        D_OUT = 256
        NEG_SLOPE = 0.2
        key = jax.random.key(seed)
        ks = jax.random.split(key, 6)
        feat = jax.random.normal(ks[0], (N_NODES, D_IN), dtype=jnp.float32)
        scale = (2.0 / (D_IN + D_OUT)) ** 0.5
        W_src = jax.random.normal(ks[1], (D_IN, D_OUT), dtype=jnp.float32) * scale
        b_src = jnp.zeros((D_OUT,), dtype=jnp.float32)
        W_dst = jax.random.normal(ks[2], (D_IN, D_OUT), dtype=jnp.float32) * scale
        b_dst = jnp.zeros((D_OUT,), dtype=jnp.float32)
        attn = jax.random.normal(ks[3], (D_OUT,), dtype=jnp.float32) * scale
        src = jax.random.randint(ks[4], (N_EDGES,), 0, N_NODES, dtype=jnp.int32)
        dst = jax.random.randint(ks[5], (N_EDGES,), 0, N_NODES, dtype=jnp.int32)
        return {'feat': feat, 'W_src': W_src, 'b_src': b_src, 'W_dst': W_dst, 'b_dst': b_dst, 'attn': attn, 'src': src, 'dst': dst}
    _L0_gnn_all = _L0_gnn_setup()
    _L0_gnn_in = {k: v for k, v in _L0_gnn_all.items() if k in ('W_src', 'b_src', 'W_dst', 'b_dst', 'attn')}
    del _L0_gnn_all

    def _L0_mix_setup():
        import jax, jax.numpy as jnp
        import numpy as np
        C_CURV = 1.0
        MIN_NORM = 1e-15
        BALL_EPS = 1e-05
        ATT_EPS = 1e-15
        DIM = 32

        def _norm(x):
            return jnp.clip(jnp.linalg.norm(x, axis=-1, keepdims=True), MIN_NORM)

        def proj(x, c):
            maxnorm = (1.0 - BALL_EPS) / jnp.sqrt(c)
            n = _norm(x)
            return jnp.where(n > maxnorm, x / n * maxnorm, x)

        def expmap0(u, c):
            sc = jnp.sqrt(c)
            n = _norm(u)
            return jnp.tanh(sc * n) * u / (sc * n)

        def logmap0(p, c):
            sc = jnp.sqrt(c)
            n = _norm(p)
            return jnp.arctanh(jnp.clip(sc * n, -1.0 + 1e-07, 1.0 - 1e-07)) * p / (sc * n)

        def mobius_add(x, y, c):
            x2 = jnp.sum(x * x, -1, keepdims=True)
            y2 = jnp.sum(y * y, -1, keepdims=True)
            xy = jnp.sum(x * y, -1, keepdims=True)
            num = (1 + 2 * c * xy + c * y2) * x + (1 - c * x2) * y
            den = 1 + 2 * c * xy + c * c * x2 * y2
            return num / jnp.clip(den, MIN_NORM)

        def conv1d(x, w, pad, groups=1):
            return jax.lax.conv_general_dilated(x, w, (1,), [(pad, pad)], dimension_numbers=('NCH', 'OIH', 'NCH'), feature_group_count=groups)

        def batchnorm(x, gamma, beta):
            mean = jnp.mean(x, axis=(0, 2), keepdims=True)
            var = jnp.var(x, axis=(0, 2), keepdims=True)
            xn = (x - mean) * jax.lax.rsqrt(var + 1e-05)
            return gamma[None, :, None] * xn + beta[None, :, None]

        def _reference_tuple_inner(x, w_qkv, bn_gamma, bn_beta, w_dw, w_pw, w_res, b_res):
            c = C_CURV
            h = logmap0(proj(x, c), c)
            h = jnp.transpose(h, (1, 2, 0))
            h = conv1d(h, w_qkv, pad=2)
            h = batchnorm(h, bn_gamma, bn_beta)
            h = jax.nn.relu(jnp.transpose(h, (2, 0, 1)))
            qkv = proj(expmap0(h, c), c)
            t = jnp.transpose(logmap0(proj(qkv, c), c), (1, 2, 0))
            s = conv1d(t, w_dw, pad=2, groups=t.shape[1])
            s = conv1d(s, w_pw, pad=0, groups=t.shape[1] // DIM)
            cat = jnp.concatenate([t, s], axis=1)
            ai = proj(expmap0(jnp.transpose(cat, (2, 0, 1)), c), c)
            t2 = logmap0(proj(ai, c), c)
            L, N, C2 = t2.shape
            g = C2 // (3 * DIM)
            qkv3 = jnp.transpose(t2, (1, 2, 0)).reshape(N, g, 3 * DIM, L)
            q, k, v = jnp.split(qkv3, 3, axis=2)
            q = jax.nn.relu(q)
            k = jax.nn.relu(k)
            vk = jnp.einsum('ngdl,ngel->ngde', v, k)
            out = jnp.einsum('ngde,ngdl->ngdl', vk, q)
            out = out / (jnp.sum(v, -1, keepdims=True) + ATT_EPS)
            out = jnp.transpose(out.reshape(N, g * DIM, L), (2, 0, 1))
            fx_h = proj(expmap0(out, c), c)
            ft = jnp.transpose(logmap0(proj(fx_h, c), c), (1, 2, 0))
            ft = conv1d(ft, w_res, pad=0) + b_res[None, :, None]
            fx = proj(expmap0(jnp.transpose(ft, (2, 0, 1)), c), c)
            residual = mobius_add(fx, x, c)
            return (fx, residual)
        key = jax.random.key(seed)
        ks = jax.random.split(key, 6)
        L, N, C, TD = (256, 16, 256, 256)
        x = jax.random.normal(ks[0], (L, N, C), jnp.float32) * 0.05
        w_qkv = jax.random.normal(ks[1], (3 * TD, C, 5), jnp.float32) / np.sqrt(C * 5)
        bn_gamma = jnp.ones((3 * TD,), jnp.float32)
        bn_beta = jnp.zeros((3 * TD,), jnp.float32)
        w_dw = jax.random.normal(ks[2], (3 * TD, 1, 5), jnp.float32) / np.sqrt(5.0)
        w_pw = jax.random.normal(ks[3], (3 * TD, DIM, 1), jnp.float32) / np.sqrt(DIM)
        w_res = jax.random.normal(ks[4], (C, 2 * TD, 1), jnp.float32) / np.sqrt(2 * TD)
        b_res = jnp.zeros((C,), jnp.float32)
        return {'x': x, 'w_qkv': w_qkv, 'bn_gamma': bn_gamma, 'bn_beta': bn_beta, 'w_dw': w_dw, 'w_pw': w_pw, 'w_res': w_res, 'b_res': b_res}
    _L0_mix_all = _L0_mix_setup()
    _L0_mix_in = {k: v for k, v in _L0_mix_all.items() if k in ('w_qkv', 'bn_gamma', 'bn_beta', 'w_dw', 'w_pw', 'w_res', 'b_res')}
    del _L0_mix_all

    def _L0_ffn_setup():
        import math
        import jax, jax.numpy as jnp
        import numpy as np
        CAPACITY_FACTOR = 1.25
        key = jax.random.key(seed)
        ks = jax.random.split(key, 5)
        B, L, D, F, E = (8, 1024, 256, 1024, 8)
        h = jax.random.normal(ks[0], (B, L, D), dtype=jnp.float32)
        gate_w = jax.random.normal(ks[1], (D, E), dtype=jnp.float32) * 0.02
        gate_b = jnp.zeros((E,), dtype=jnp.float32)
        w1 = jax.random.normal(ks[2], (E, D, F), dtype=jnp.float32) * (1.0 / math.sqrt(D))
        b1 = jnp.zeros((E, F), dtype=jnp.float32)
        w2 = jax.random.normal(ks[3], (E, F, D), dtype=jnp.float32) * (1.0 / math.sqrt(F))
        b2 = jnp.zeros((E, D), dtype=jnp.float32)
        return {'h': h, 'gate_w': gate_w, 'gate_b': gate_b, 'w1': w1, 'b1': b1, 'w2': w2, 'b2': b2}
    _L0_ffn_all = _L0_ffn_setup()
    _L0_ffn_in = {k: v for k, v in _L0_ffn_all.items() if k in ('gate_w', 'gate_b', 'w1', 'b1', 'w2', 'b2')}
    del _L0_ffn_all
    return {'x': x, 'src': src, 'dst': dst, 'L0_gnn_W_src': _L0_gnn_in['W_src'], 'L0_gnn_b_src': _L0_gnn_in['b_src'], 'L0_gnn_W_dst': _L0_gnn_in['W_dst'], 'L0_gnn_b_dst': _L0_gnn_in['b_dst'], 'L0_gnn_attn': _L0_gnn_in['attn'], 'L0_mix_w_qkv': _L0_mix_in['w_qkv'], 'L0_mix_bn_gamma': _L0_mix_in['bn_gamma'], 'L0_mix_bn_beta': _L0_mix_in['bn_beta'], 'L0_mix_w_dw': _L0_mix_in['w_dw'], 'L0_mix_w_pw': _L0_mix_in['w_pw'], 'L0_mix_w_res': _L0_mix_in['w_res'], 'L0_mix_b_res': _L0_mix_in['b_res'], 'L0_ffn_gate_w': _L0_ffn_in['gate_w'], 'L0_ffn_gate_b': _L0_ffn_in['gate_b'], 'L0_ffn_w1': _L0_ffn_in['w1'], 'L0_ffn_b1': _L0_ffn_in['b1'], 'L0_ffn_w2': _L0_ffn_in['w2'], 'L0_ffn_b2': _L0_ffn_in['b2']}

def reference(x, src, dst, L0_gnn_W_src, L0_gnn_b_src, L0_gnn_W_dst, L0_gnn_b_dst, L0_gnn_attn, L0_mix_w_qkv, L0_mix_bn_gamma, L0_mix_bn_beta, L0_mix_w_dw, L0_mix_w_pw, L0_mix_w_res, L0_mix_b_res, L0_ffn_gate_w, L0_ffn_gate_b, L0_ffn_w1, L0_ffn_b1, L0_ffn_w2, L0_ffn_b2):
    import jax
    import jax.numpy as jnp

    def _L0_gnn_ref(feat, W_src, b_src, W_dst, b_dst, attn, src, dst):
        import jax, jax.numpy as jnp
        import numpy as np
        N_NODES = 12500
        N_EDGES = 37500
        D_IN = 256
        D_OUT = 256
        NEG_SLOPE = 0.2
        N = feat.shape[0]
        el = feat @ W_src + b_src
        er = feat @ W_dst + b_dst
        e = jax.nn.leaky_relu(el[src] + er[dst], NEG_SLOPE)
        score = e @ attn
        smax = jax.ops.segment_max(score, dst, num_segments=N)
        ex = jnp.exp(score - smax[dst])
        ssum = jax.ops.segment_sum(ex, dst, num_segments=N)
        a = ex / ssum[dst]
        out = jax.ops.segment_sum(el[src] * a[:, None], dst, num_segments=N)
        return out

    def _L0_mix_ref(x, w_qkv, bn_gamma, bn_beta, w_dw, w_pw, w_res, b_res):
        import jax, jax.numpy as jnp
        import numpy as np
        C_CURV = 1.0
        MIN_NORM = 1e-15
        BALL_EPS = 1e-05
        ATT_EPS = 1e-15
        DIM = 32

        def _norm(x):
            return jnp.clip(jnp.linalg.norm(x, axis=-1, keepdims=True), MIN_NORM)

        def proj(x, c):
            maxnorm = (1.0 - BALL_EPS) / jnp.sqrt(c)
            n = _norm(x)
            return jnp.where(n > maxnorm, x / n * maxnorm, x)

        def expmap0(u, c):
            sc = jnp.sqrt(c)
            n = _norm(u)
            return jnp.tanh(sc * n) * u / (sc * n)

        def logmap0(p, c):
            sc = jnp.sqrt(c)
            n = _norm(p)
            return jnp.arctanh(jnp.clip(sc * n, -1.0 + 1e-07, 1.0 - 1e-07)) * p / (sc * n)

        def mobius_add(x, y, c):
            x2 = jnp.sum(x * x, -1, keepdims=True)
            y2 = jnp.sum(y * y, -1, keepdims=True)
            xy = jnp.sum(x * y, -1, keepdims=True)
            num = (1 + 2 * c * xy + c * y2) * x + (1 - c * x2) * y
            den = 1 + 2 * c * xy + c * c * x2 * y2
            return num / jnp.clip(den, MIN_NORM)

        def conv1d(x, w, pad, groups=1):
            return jax.lax.conv_general_dilated(x, w, (1,), [(pad, pad)], dimension_numbers=('NCH', 'OIH', 'NCH'), feature_group_count=groups)

        def batchnorm(x, gamma, beta):
            mean = jnp.mean(x, axis=(0, 2), keepdims=True)
            var = jnp.var(x, axis=(0, 2), keepdims=True)
            xn = (x - mean) * jax.lax.rsqrt(var + 1e-05)
            return gamma[None, :, None] * xn + beta[None, :, None]

        def _reference_tuple_inner(x, w_qkv, bn_gamma, bn_beta, w_dw, w_pw, w_res, b_res):
            c = C_CURV
            h = logmap0(proj(x, c), c)
            h = jnp.transpose(h, (1, 2, 0))
            h = conv1d(h, w_qkv, pad=2)
            h = batchnorm(h, bn_gamma, bn_beta)
            h = jax.nn.relu(jnp.transpose(h, (2, 0, 1)))
            qkv = proj(expmap0(h, c), c)
            t = jnp.transpose(logmap0(proj(qkv, c), c), (1, 2, 0))
            s = conv1d(t, w_dw, pad=2, groups=t.shape[1])
            s = conv1d(s, w_pw, pad=0, groups=t.shape[1] // DIM)
            cat = jnp.concatenate([t, s], axis=1)
            ai = proj(expmap0(jnp.transpose(cat, (2, 0, 1)), c), c)
            t2 = logmap0(proj(ai, c), c)
            L, N, C2 = t2.shape
            g = C2 // (3 * DIM)
            qkv3 = jnp.transpose(t2, (1, 2, 0)).reshape(N, g, 3 * DIM, L)
            q, k, v = jnp.split(qkv3, 3, axis=2)
            q = jax.nn.relu(q)
            k = jax.nn.relu(k)
            vk = jnp.einsum('ngdl,ngel->ngde', v, k)
            out = jnp.einsum('ngde,ngdl->ngdl', vk, q)
            out = out / (jnp.sum(v, -1, keepdims=True) + ATT_EPS)
            out = jnp.transpose(out.reshape(N, g * DIM, L), (2, 0, 1))
            fx_h = proj(expmap0(out, c), c)
            ft = jnp.transpose(logmap0(proj(fx_h, c), c), (1, 2, 0))
            ft = conv1d(ft, w_res, pad=0) + b_res[None, :, None]
            fx = proj(expmap0(jnp.transpose(ft, (2, 0, 1)), c), c)
            residual = mobius_add(fx, x, c)
            return (fx, residual)
        return _reference_tuple_inner(x, w_qkv, bn_gamma, bn_beta, w_dw, w_pw, w_res, b_res)[0]

    def _L0_ffn_ref(h, gate_w, gate_b, w1, b1, w2, b2):
        import math
        import jax, jax.numpy as jnp
        import numpy as np
        CAPACITY_FACTOR = 1.25
        B, L, D = h.shape
        E = gate_w.shape[1]
        T = B * L
        C = max(1, math.ceil(CAPACITY_FACTOR * T / E))
        x = h.reshape(T, D)
        logits = x @ gate_w + gate_b
        probs = jax.nn.softmax(logits, axis=-1)
        idx = jnp.argmax(probs, axis=-1)
        prb = jnp.take_along_axis(probs, idx[:, None], axis=1)[:, 0]
        one_hot = jax.nn.one_hot(idx, E, dtype=jnp.float32)
        pos = (jnp.cumsum(one_hot, axis=0) * one_hot).sum(-1).astype(jnp.int32) - 1
        kept = pos < C
        pos_safe = jnp.where(kept, pos, C)
        buf = jnp.zeros((E, C, D), dtype=h.dtype).at[idx, pos_safe].set(x, mode='drop')
        hmid = jax.nn.relu(jnp.einsum('ecd,edf->ecf', buf, w1) + b1[:, None, :])
        ybuf = jnp.einsum('ecf,efd->ecd', hmid, w2) + b2[:, None, :]
        pos_g = jnp.minimum(pos, C - 1)
        y_tok = ybuf[idx, pos_g] * (prb * kept)[:, None]
        y = y_tok.reshape(B, L, D)
        y = jnp.nan_to_num(y, nan=0.0, posinf=10000.0, neginf=-10000.0)
        return y
    xn = _layernorm(x, axis=-1)
    x = x + _L0_gnn_ref(xn, L0_gnn_W_src, L0_gnn_b_src, L0_gnn_W_dst, L0_gnn_b_dst, L0_gnn_attn, src, dst) + _L0_mix_ref(xn[None], L0_mix_w_qkv, L0_mix_bn_gamma, L0_mix_bn_beta, L0_mix_w_dw, L0_mix_w_pw, L0_mix_w_res, L0_mix_b_res)[0]
    x = x + _L0_ffn_ref(_layernorm(x, axis=-1)[None], L0_ffn_gate_w, L0_ffn_gate_b, L0_ffn_w1, L0_ffn_b1, L0_ffn_w2, L0_ffn_b2)[0]
    return x

_drawn_inputs = setup_inputs


def setup_inputs(seed=0):
    import zlib

    import numpy as np

    out = dict(_drawn_inputs(seed))
    spreads = {'L0_gnn_b_src': (0.0, 0.1),
     'L0_gnn_b_dst': (0.0, 0.633),
     'L0_mix_bn_gamma': (1.0, 0.6),
     'L0_mix_bn_beta': (0.0, 0.337),
     'L0_mix_b_res': (0.0, 0.291),
     'L0_ffn_gate_b': (0.0, 0.1),
     'L0_ffn_b1': (0.0, 0.619),
     'L0_ffn_b2': (0.0, 0.44)}
    factors = {'L0_mix_w_dw': 4.62, 'L0_mix_w_pw': 4.288}
    for name, (base, spread) in spreads.items():
        noise = np.random.default_rng([zlib.crc32(name.encode()), seed]).standard_normal(out[name].shape)
        drawn = base * np.exp(spread * noise) if base else spread * noise
        out[name] = jnp.asarray(drawn.astype(out[name].dtype))
    for name, factor in factors.items():
        out[name] = (out[name] * factor).astype(out[name].dtype)
    return out
```

```python
from contextlib import ExitStack

import numpy as np

import concourse.bass as bass
from concourse import mybir

NODES, EDGES, D = 6250, 200000, 256
P = 128
CH = 4
CHUNKS = -(-NODES // (P * CH))
TILES = CH * CHUNKS
ROWS = TILES * P
WINDOWS = -(-NODES // P)
QKV = 768
CT = QKV // P
HEADS, HD = 16, 32
OUT3 = HEADS * HD
KD = D // P
GE = CH * P
GROUPS = -(-EDGES // GE)
ROW_T = D + 2
STEPS_MAX = GROUPS * WINDOWS + 4
STEP_COLS = -(-STEPS_MAX // P)
RING = 4
EXPERTS, FF = 8, 1024
CAP = -(-(5 * NODES) // (4 * EXPERTS))
TT = 123
ET = 8
SLOTS = TT * ET
FT = FF // P
NO_NODE = 16383
NO_SLOT = 1 << 20

LN_EPS = 1e-5
MIN_NORM = 1e-15
MAX_NORM = float(np.float32(1.0) - np.float32(1e-5))
RADIUS = float(np.arctanh(np.float64(np.float32(MAX_NORM))))
BIG = float(2.0 ** 100)
SLOPE = 0.2

F32, I32, U32 = mybir.dt.float32, mybir.dt.int32, mybir.dt.uint32
ALU = mybir.AluOpType
ACT = mybir.ActivationFunctionType
X = mybir.AxisListType.X


def ds(start, size):
    return bass.ds(start, size)


class Order:

    def __init__(self, eng, sem, base=0):
        self.eng, self.sem, self.base, self.n = eng, sem, base, 0

    def then(self, ins):
        ins.then_inc(self.sem, 1)
        self.n += 1
        self.eng.wait_ge(self.sem, self.base + self.n)


def wait_apart(eng, sem, value, met):
    value = eng.to_reg(value)
    eng.wait_ge(*met)
    eng.wait_ge(sem, value)


def row_statistics(nc, sems, st, x_rows, a, room):
    x_in, stats_done, v, s_act = sems("x_in0", "stats_done", "s1_vector", "s1_scalar")
    x_all = room[:, :, :].rearrange("p a b -> p (a b)")[:, 0:TILES * D].rearrange("p (t d) -> p t d", d=D)
    with nc.Block() as block:
        @block.sync
        def _(sp):
            sp.dma_start(x_all[:, :, :], x_rows).then_inc(x_in, 16)

        @block.vector
        def _(dve):
            dve.wait_ge(x_in, 16)
            with dve.Fori(0, TILES) as t:
                nc.vector.bn_stats(st[:, ds(t, 1), :], x_all[:, ds(t, 1), :]).then_inc(stats_done, 1)
            dve.wait_ge(stats_done, TILES)
            row_moments(nc, dve, v, st, a, TILES)
            then = Order(dve, v, MOMENT_OPS).then
            then(nc.vector.tensor_scalar(a["var_c"], a["var"], 1e-30, None, ALU.max))
            dve.wait_ge(s_act, 2)
            then(nc.vector.reciprocal(a["rstd"], a["sd"]))
            then(nc.vector.tensor_tensor(a["n"], a["sv"], a["rstd"], ALU.mult))
            then(nc.vector.tensor_scalar(a["n"], a["n"], float(D) ** 0.5, MIN_NORM, ALU.mult, ALU.max))
            then(nc.vector.tensor_scalar(a["nm"], a["n"], MAX_NORM, None, ALU.min))
            then(nc.vector.tensor_scalar(a["t0"], a["nm"], -1.0, 1.0, ALU.mult, ALU.add))
            then(nc.vector.reciprocal(a["t0"], a["t0"]))
            then(nc.vector.tensor_scalar(a["t1"], a["nm"], 1.0, None, ALU.add))
            then(nc.vector.tensor_tensor(a["ratio"], a["t0"], a["t1"], ALU.mult))
            then(nc.vector.tensor_tensor(a["t0"], a["nm"], a["nm"], ALU.mult))
            then(nc.vector.tensor_scalar(a["t1"], a["t0"], 1 / 11, 1 / 9, ALU.mult, ALU.add))
            for k in (7, 5, 3, 1):
                then(nc.vector.tensor_tensor(a["t1"], a["t1"], a["t0"], ALU.mult))
                then(nc.vector.tensor_scalar(a["t1"], a["t1"], 1 / k, None, ALU.add))
            then(nc.vector.tensor_tensor(a["t1"], a["t1"], a["nm"], ALU.mult))
            dve.wait_ge(s_act, 3)
            then(nc.vector.tensor_scalar(a["t2"], a["log"], 0.5, None, ALU.mult))
            then(nc.vector.tensor_tensor(a["t1"], a["t1"], a["t2"], ALU.subtract))
            then(nc.vector.tensor_scalar(a["t0"], a["nm"], 0.25, None, ALU.is_lt))
            then(nc.vector.tensor_tensor(a["t1"], a["t1"], a["t0"], ALU.mult))
            then(nc.vector.tensor_tensor(a["t1"], a["t1"], a["t2"], ALU.add))
            then(nc.vector.reciprocal(a["t0"], a["n"]))
            then(nc.vector.tensor_tensor(a["logmap"], a["t0"], a["t1"], ALU.mult))

        @block.scalar
        def _(act):
            act.wait_ge(v, MOMENT_OPS)
            nc.scalar.activation(a["sd"], a["var_e"], ACT.Sqrt).then_inc(s_act, 1)
            act.wait_ge(v, MOMENT_OPS + 1)
            nc.scalar.activation(a["sv"], a["var_c"], ACT.Sqrt).then_inc(s_act, 1)
            act.wait_ge(v, MOMENT_OPS + 9)
            nc.scalar.activation(a["log"], a["ratio"], ACT.Ln).then_inc(s_act, 1)


MOMENT_OPS = 8


def row_moments(nc, dve, sem, st, a, n):
    o = Order(dve, sem)
    o.then(nc.vector.tensor_tensor(a["mean"][:, 0:n], st[:, 0:n, 1], st[:, 0:n, 4], ALU.add))
    o.then(nc.vector.tensor_scalar(a["mean"][:, 0:n], a["mean"][:, 0:n], 0.5, None, ALU.mult))
    o.then(nc.vector.tensor_tensor(a["t0"][:, 0:n], st[:, 0:n, 1], st[:, 0:n, 4], ALU.subtract))
    o.then(nc.vector.tensor_tensor(a["t0"][:, 0:n], a["t0"][:, 0:n], a["t0"][:, 0:n], ALU.mult))
    o.then(nc.vector.tensor_tensor(a["t1"][:, 0:n], st[:, 0:n, 2], st[:, 0:n, 5], ALU.add))
    o.then(nc.vector.scalar_tensor_tensor(a["var"][:, 0:n], a["t0"][:, 0:n], D / 4, a["t1"][:, 0:n], ALU.mult, ALU.add))
    o.then(nc.vector.tensor_scalar(a["var"][:, 0:n], a["var"][:, 0:n], 1 / D, None, ALU.mult))
    o.then(nc.vector.tensor_scalar(a["var_e"][:, 0:n], a["var"][:, 0:n], LN_EPS, None, ALU.add))
    assert o.n == MOMENT_OPS


def project(nc, sems, x_rows, w, a, ident, hT, hst, el_rows, er_rows):
    x_in = sems(*(f"x_in1_{j}" for j in range(CH)))
    row_out, rows_stored = sems("row_out", "rows_stored")
    w_in, xn_ready, tp_ready, copied, sd_ready, rows_added, rows_ready, h_ready, h_kept = sems(
        "w_in1", "xn_ready", "tp_ready", "copied", "sd_ready", "rows_added", "rows_ready", "h_ready", "h_kept")
    with ExitStack() as ctx:
        sb, ps = allocators(nc, ctx)
        xb = sb("xb1", [P, CH, D])
        xn = sb("xn", [P, 2, 2, D])
        xnT = sb("xnT", [P, 2, KD, P])
        hinT = sb("hinT", [P, KD, GE])
        w_sd = sb("w_sd", [P, KD, 2 * D])
        w_qkv = sb("w_qkv", [P, KD, QKV])
        b_sd = sb("b_sd", [P, 2, D])
        attn_b = sb("attn_b1", [P, D])
        rows = sb("rows", [P, 2, 2, ROW_T])
        junk = sb("junk1", [P, D])
        tp = ps("tp", [P, 2, 4, P])
        sd_ps = ps("sd_ps", [P, 2, 2 * D])
        h_ps = ps("h_ps", [P, 2, GE])
        block = ctx.enter_context(nc.Block())

        @block.sync
        def _(sp):
            sp.dma_start(w_sd[:, :, 0:D], w["W_src"].rearrange("(k p) n -> p k n", p=P)).then_inc(w_in, 16)
            sp.dma_start(w_sd[:, :, D:2 * D], w["W_dst"].rearrange("(k p) n -> p k n", p=P)).then_inc(w_in, 16)
            sp.dma_start(w_qkv[:, :, :], w["w_qkv"].rearrange("(k p) n -> p k n", p=P)).then_inc(w_in, 16)
            sp.dma_start(b_sd[:, 0, :], w["b_src"].partition_broadcast(P)).then_inc(w_in, 16)
            sp.dma_start(b_sd[:, 1, :], w["b_dst"].partition_broadcast(P)).then_inc(w_in, 16)
            sp.dma_start(attn_b[:, :], w["attn"].partition_broadcast(P)).then_inc(w_in, 16)
            with sp.Fori(0, CHUNKS) as i:
                for j in range(CH):
                    sp.wait_ge(xn_ready, (i * CH + j) * 2 + 1)
                    sp.dma_start(xb[:, j, :], x_rows[:, ds(i * CH + j, 1), :]).then_inc(x_in[j], 16)

        @block.vector
        def _(dve):
            dve.sem_inc(xn_ready, 2 * CH)
            dve.sem_inc(rows_added, 2)
            for j in range(2):
                nc.vector.memset(rows[:, j, :, D + 1:D + 2], 1.0)
            dve.wait_ge(w_in, 96)
            with dve.Fori(0, CHUNKS) as i:
                for j in range(CH):
                    t = i * CH + j
                    dve.wait_ge(x_in[j], i * 16 + 16)
                    dve.wait_ge(tp_ready, t + 1)
                    nc.vector.tensor_scalar(xn[:, j % 2, 0, :], xb[:, j, :], a["mean"][:, ds(t, 1)],
                                            a["rstd"][:, ds(t, 1)], ALU.subtract, ALU.mult).then_inc(xn_ready, 1)
                    dve.wait_ge(xn_ready, 2 * CH + 2 * t + 1)
                    nc.vector.tensor_scalar(xn[:, j % 2, 1, :], xn[:, j % 2, 0, :], a["logmap"][:, ds(t, 1)],
                                            None, ALU.mult).then_inc(xn_ready, 1)
                for j in range(CH):
                    t = i * CH + j
                    dve.wait_ge(sd_ready, 2 + t + 1)
                    dve.wait_ge(rows_stored, t + 1)
                    nc.vector.tensor_tensor(rows[:, j % 2, :, 0:D], sd_ps[:, j % 2, :].rearrange("p (a d) -> p a d", a=2),
                                            b_sd[:, :, :], ALU.add).then_inc(rows_added, 1)
                    dve.wait_ge(rows_added, 2 + t + 1)
                    for s in range(2):
                        nc.vector.scalar_tensor_tensor(junk[:, :], rows[:, j % 2, s, 0:D], SLOPE, attn_b[:, :], ALU.mult,
                                                       ALU.mult, accum_out=rows[:, j % 2, s, D:D + 1]).then_inc(rows_ready, 1)
                        dve.wait_ge(rows_ready, t * 2 + s + 1)
                for c in range(CT):
                    dve.wait_ge(h_kept, 2 + i * CT + c + 1)
                    nc.vector.bn_stats(hst[:, c, ds(i, 1), :], hT[:, c, ds(i * GE, GE)])

        @block.gpsimd
        def _(pool):
            pool.sem_inc(rows_stored, 2)
            with pool.Fori(0, CHUNKS) as i:
                for j in range(CH):
                    t = i * CH + j
                    pool.wait_ge(rows_ready, t * 2 + 2)
                    pool.dma_start(el_rows[:, ds(t, 1), :], rows[:, j % 2, 0, :]).then_inc(row_out, 16)
                    pool.dma_start(er_rows[:, ds(t, 1), :], rows[:, j % 2, 1, :]).then_inc(row_out, 16)
                    pool.wait_ge(row_out, t * 32 + 32)
                    pool.sem_inc(rows_stored, 1)

        @block.tensor
        def _(pe):
            pe.sem_inc(tp_ready, 2)
            pe.sem_inc(sd_ready, 2)
            pe.sem_inc(h_ready, 1)
            pe.wait_ge(w_in, 96)

            def products(i, j):
                t = i * CH + j
                pe.wait_ge(copied, 4 + 2 * t + 2)
                pe.wait_ge(rows_added, t + 1)
                for k in range(KD):
                    last = nc.tensor.matmul(sd_ps[:, j % 2, :], xnT[:, j % 2, k, :], w_sd[:, k, :], start=(k == 0), stop=(k == KD - 1))
                last.then_inc(sd_ready, 1)

            with pe.Fori(0, CHUNKS) as i:
                for j in range(CH):
                    t = i * CH + j
                    pe.wait_ge(xn_ready, 2 * CH + 2 * t + 2)
                    pe.wait_ge(copied, 2 * t + 2)
                    for k in range(4):
                        last = nc.tensor.transpose(tp[:, j % 2, k, :], xn[:, j % 2, k // 2, (k % 2) * P:(k % 2) * P + P], ident)
                    last.then_inc(tp_ready, 1)
                    if j:
                        products(i, j - 1)
                products(i, CH - 1)
                for c in range(CT):
                    pe.wait_ge(h_kept, i * CT + c + 1)
                    for k in range(KD):
                        last = nc.tensor.matmul(h_ps[:, c % 2, :], w_qkv[:, k, c * P:(c + 1) * P], hinT[:, k, :],
                                                start=(k == 0), stop=(k == KD - 1))
                    last.then_inc(h_ready, 1)

        @block.scalar
        def _(act):
            act.sem_inc(copied, 4)
            act.sem_inc(h_kept, 2)
            with act.Fori(0, CHUNKS) as i:
                for j in range(CH):
                    t = i * CH + j
                    act.wait_ge(tp_ready, 2 + t + 1)
                    if j == 0:
                        act.wait_ge(h_ready, i * CT + 1)
                    nc.scalar.activation(hinT[:, :, j * P:(j + 1) * P], tp[:, j % 2, 2:4, :], ACT.Copy).then_inc(copied, 1)
                    act.wait_ge(sd_ready, t + 1)
                    nc.scalar.activation(xnT[:, j % 2, :, :], tp[:, j % 2, 0:2, :], ACT.Copy).then_inc(copied, 1)
                for c in range(CT):
                    act.wait_ge(h_ready, 1 + i * CT + c + 1)
                    nc.scalar.activation(hT[:, c, ds(i * GE, GE)], h_ps[:, c % 2, :], ACT.Copy).then_inc(h_kept, 1)


def batch_norm(nc, sems, hst, gb, gamma_in, beta_in, b):
    v, s_act, gb_in = sems("s3_vector", "s3_scalar", "gb_in")
    gamma, beta = gb[:, 0, :], gb[:, 1, :]
    r = ROWS / NODES
    with nc.Block() as block:
        @block.vector
        def _(dve):
            o = Order(dve, v)
            for c in range(CT):
                nc.vector.bn_aggr(b["agg"][:, c, :], hst[:, c, :, :]).then_inc(v, 1)
            o.n = CT
            dve.wait_ge(v, CT)
            o.then(nc.vector.tensor_tensor(b["t0"], b["agg"][:, :, 0], b["agg"][:, :, 0], ALU.mult))
            o.then(nc.vector.tensor_scalar(b["t0"], b["t0"], r - r * r, LN_EPS, ALU.mult, ALU.add))
            o.then(nc.vector.scalar_tensor_tensor(b["t1"], b["agg"][:, :, 1], r, b["t0"], ALU.mult, ALU.add))
            dve.wait_ge(s_act, 1)
            dve.wait_ge(gb_in, 32)
            o.then(nc.vector.reciprocal(b["t0"], b["t2"]))
            o.then(nc.vector.tensor_tensor(b["scale"], b["t0"], gamma, ALU.mult))
            o.then(nc.vector.tensor_tensor(b["t1"], b["agg"][:, :, 0], b["scale"], ALU.mult))
            o.then(nc.vector.tensor_scalar(b["t1"], b["t1"], r, None, ALU.mult))
            o.then(nc.vector.tensor_tensor(b["shift"], beta, b["t1"], ALU.subtract))

        @block.sync
        def _(sp):
            sp.dma_start(gamma, gamma_in).then_inc(gb_in, 16)
            sp.dma_start(beta, beta_in).then_inc(gb_in, 16)

        @block.scalar
        def _(act):
            act.wait_ge(v, CT + 3)
            nc.scalar.activation(b["t2"], b["t1"], ACT.Sqrt).then_inc(s_act, 1)


def allocators(nc, ctx):
    def sb(name, shape, dt=F32):
        return ctx.enter_context(nc.sbuf_tensor(name, shape, dt))

    def ps(name, shape, dt=F32):
        return ctx.enter_context(nc.psum_tensor(name, shape, dt))
    return sb, ps


def program(nc, t, out):
    names = []

    def sems(*wanted):
        names.extend(wanted)
        return [outer.enter_context(nc.semaphore(n)) for n in wanted] if len(wanted) > 1 else [outer.enter_context(nc.semaphore(wanted[0]))]

    el_tab = nc.dram_tensor("el_tab", [ROWS, ROW_T], F32).ap()
    er_tab = nc.dram_tensor("er_tab", [ROWS, ROW_T], F32).ap()
    x_mix = nc.dram_tensor("x_mix", [ROWS, D], F32).ap()
    moe_in = nc.dram_tensor("moe_in", [EXPERTS * SLOTS, D], F32).ap()
    moe_out = nc.dram_tensor("moe_out", [EXPERTS * SLOTS, D], F32).ap()
    by_tile = lambda ap: ap.rearrange("(t p) d -> p t d", p=P)
    with ExitStack() as outer:
        sb, ps = allocators(nc, outer)
        ident_t = sb("ident", [P, P])
        ident = ident_t[:, :]
        constants(nc, sems, ident)
        with ExitStack() as early:
            sbe, ps = allocators(nc, early)
            hT = sbe("hT", [P, CT, ROWS])
            hst = sbe("hst", [P, CT, CHUNKS, 6])
            stats = sbe("row_stats", [P, 20, TILES])
            a = {n: stats[:, k, :] for k, n in enumerate((
                "mean", "rstd", "logmap", "var", "var_e", "var_c", "sd", "sv", "n", "nm", "ratio", "log", "t0", "t1", "t2"))}
            with nc.sbuf_tensor("row_bn", [P, TILES, 6], F32) as st:
                row_statistics(nc, sems, st, by_tile(t["x"]), a, hT)
            project(nc, sems, by_tile(t["x"]), t, a, ident, hT, hst, by_tile(el_tab), by_tile(er_tab))
            gb = sbe("gamma_beta", [P, 2, CT])
            bn = sbe("bn", [P, 8, CT])
            b = {n: bn[:, k, :] for k, n in enumerate(("t0", "t1", "t2", "scale", "shift"))}
            b["agg"] = sbe("agg", [P, CT, 2])
            ss3 = sbe("ss3", [P, TILES])
            batch_norm(nc, sems, hst, gb, t["gamma"], t["beta"], b)
            normalise_h(nc, sems, hT, b)
            mixer(nc, sems, t, ident, hT, ss3)
            mixer_out(nc, sems, t, hT, ss3, by_tile(t["x"]), by_tile(x_mix))
        cum_row = sb("cum_row", [1, RING_GROUPS], I32)
        acc = sb("acc", [P, REAL_WINDOWS, ROW_T])
        negm_all = sb("negm_all", [P, REAL_WINDOWS])
        lists = nc.dram_tensor("group_lists", [2, 4 * P], F32).ap()
        table = nc.dram_tensor("step_table", [(STEP_COLS + 1) * P, 2], I32).ap()
        step_table(nc, sems, t["dst_rows"], lists, table, cum_row)
        attention(nc, sems, t, ident, el_tab, by_tile(er_tab), table, cum_row, acc, negm_all)
        zeros = sb("zeros", [P, D])
        st9 = sb("st9", [P, TILES, 6])
        a9 = sb("a9", [P, 8, TILES])
        a = {n: a9[:, k, :] for k, n in enumerate(("mean", "rstd", "var", "var_e", "sd", "t0", "t1"))}
        routing = {"weight": sb("weight", [P, WINDOWS])[:, :], "slot": sb("slot", [P, WINDOWS], I32)[:, :]}
        residual_sum(nc, sems, by_tile(x_mix), acc, st9, zeros, moe_in)
        route(nc, sems, t, ident, acc, st9, a, routing, moe_in)
        experts(nc, sems, t, ident, moe_in, moe_out)
        combine(nc, sems, acc, routing, zeros, moe_out, by_tile(out))


PAIRS = 2 * CHUNKS


def pipelined(eng, chunk, count):
    chunk(0)
    with eng.Fori(1, count) as i:
        chunk(i)
    chunk(count)


def valid(pair, pairs):
    return not isinstance(pair, int) or 0 <= pair < pairs


def normalise_h(nc, sems, hT, b):
    u_chain, = sems("u_chain")
    with nc.Block() as block:
        @block.scalar
        def _(act):
            for c in range(4):
                nc.scalar.activation(hT[:, c, :], hT[:, c, :], ACT.Relu, bias=b["shift"][:, c:c + 1],
                                     scale=b["scale"][:, c:c + 1])

        @block.vector
        def _(dve):
            o = Order(dve, u_chain)
            for c in range(4, CT):
                o.then(nc.vector.tensor_scalar(hT[:, c, :], hT[:, c, :], b["scale"][:, c:c + 1], b["shift"][:, c:c + 1],
                                               ALU.mult, ALU.add))
                o.then(nc.vector.tensor_scalar(hT[:, c, :], hT[:, c, :], 0.0, None, ALU.max))


def mixer(nc, sems, w, ident, uT, ss3):
    w_in, u_copied, us_ready, us_kept, squared, norms_ready, small = sems(
        "w_in5", "u_copied", "us_ready", "us_kept", "squared", "norms_ready", "small5")
    o_ready, ss3_done, oT_ready, oT_kept, ft_ready, ft_kept = sems(
        "o_ready", "ss3_done", "oT_ready", "oT_kept", "ft_ready", "ft_kept")
    with ExitStack() as ctx:
        sb, ps = allocators(nc, ctx)
        u_now = sb("u_now", [P, 2, CT, P])
        w_bd = sb("w_bd", [P, CT, P])
        w_dw = sb("w_dw", [P, CT])
        w_res = sb("w_res", [P, CH, D])
        raw = sb("raw", [P, 2, 2, 3, HEADS, HD])
        junk = sb("junk5", [P, QKV], mybir.dt.bfloat16)
        ss = sb("ss5", [P, 2, 2, 2])
        nr = sb("nr5", [P, 2, 2, 2])
        f = {n: sb(f"f5_{n}", [P, 2]) for n in ("a", "b", "c1", "n2", "c", "cc")}
        ksum = sb("ksum", [P, 2, HEADS])
        oT = sb("oT", [P, 2, CH, P])
        us_ps = ps("us_ps", [P, 2, 3, 2, D])
        oT_ps = ps("oT_ps", [P, CH, P])
        ft_ps = ps("ft_ps", [P, 2, D])
        block = ctx.enter_context(nc.Block())

        @block.sync
        def _(sp):
            sp.wait_ge(small, 1)
            for g in range(4):
                sp.dma_start(w_bd[g * HD:(g + 1) * HD, :, g * HD:(g + 1) * HD], w["w_pw"][g, :, :, :]).then_inc(w_in, 16)
            sp.dma_start(w_dw[:, :], w["w_dw"]).then_inc(w_in, 16)
            sp.dma_start(w_res[:, :, :], w["w_res"].rearrange("(k p) n -> p k n", p=P)).then_inc(w_in, 16)

        @block.gpsimd
        def _(pool):
            with pool.Fori(0, CHUNKS) as i:
                for j in range(CH):
                    pool.wait_ge(us_ready, i * CH + j + 1)
                    nc.gpsimd.tensor_copy(u_now[:, j % 2, :, :], uT[:, :, ds((i * CH + j) * P, P)]).then_inc(u_copied, 1)

        @block.tensor
        def _(pe):
            pe.sem_inc(us_ready, 2)
            pe.sem_inc(oT_ready, 4)
            pe.sem_inc(ft_ready, 2)
            pe.wait_ge(w_in, 96)
            pe.wait_ge(small, 1 + CT)

            def products(t, k):
                pe.wait_ge(u_copied, t + 1)
                pe.wait_ge(us_kept, t + 1)
                for c in range(CT):
                    at = us_ps[:, k, c // 2, 0, (c % 2) * P:(c % 2 + 1) * P]
                    nc.tensor.transpose(at, u_now[:, k, c, :], ident)
                for c in range(CT):
                    at = us_ps[:, k, c // 2, 1, (c % 2) * P:(c % 2 + 1) * P]
                    last = nc.tensor.matmul(at, u_now[:, k, c, :], w_bd[:, c, :], start=True, stop=True)
                last.then_inc(us_ready, 1)

            def project(t, h, k):
                pe.wait_ge(oT_kept, t + 1)
                for c in range(CH):
                    last = nc.tensor.transpose(oT_ps[:, c, :], raw[:, h, k, 2, c * 4:(c + 1) * 4, :], ident)
                last.then_inc(oT_ready, 1)

            def residual(t, k):
                pe.wait_ge(oT_kept, 1 + t + 1)
                for c in range(CH):
                    last = nc.tensor.matmul(ft_ps[:, k, :], oT[:, k, c, :], w_res[:, c, :], start=(c == 0), stop=(c == CH - 1))
                last.then_inc(ft_ready, 1)

            def chunk(i):
                for h in range(2):
                    q = 2 * i + h
                    if valid(q, PAIRS):
                        for k in range(2):
                            products(2 * q + k, k)
                    if valid(q - 1, PAIRS):
                        pe.wait_ge(o_ready, q)
                        for k in range(2):
                            project(2 * (q - 1) + k, 1 - h, k)
                        pe.wait_ge(ft_kept, q)
                        for k in range(2):
                            residual(2 * (q - 1) + k, k)
            pipelined(pe, chunk, CHUNKS)

        @block.scalar
        def _(act):
            act.sem_inc(us_kept, 2)
            act.sem_inc(oT_kept, 1)
            act.sem_inc(ss3_done, 4)

            def keep(q, h):
                act.wait_ge(oT_ready, 2 * q + 2)
                act.wait_ge(ss3_done, 2 * q + 2)
                for k in range(2):
                    t = 2 * q + k
                    act.wait_ge(us_ready, 2 + t + 1)
                    nc.scalar.activation(raw[:, h, k, :, :, :].rearrange("p c g d -> p (c g d)"),
                                         us_ps[:, k, :, :, :].rearrange("p c s d -> p (c s d)"), ACT.Copy).then_inc(us_kept, 1)
                    act.wait_ge(us_kept, 2 + t + 1)
                    for s in range(2):
                        part = raw[:, h, k, :, s * 8:(s + 1) * 8, :].rearrange("p c g d -> p c (g d)")
                        if k == 0 and s == 0:
                            act.wait_ge(norms_ready, 3 * q + 1)
                        nc.scalar.activation(junk[:, :].rearrange("p (c n) -> p c n", c=3), part, ACT.Square, accum_out=ss[:, h, s, k:k + 1]).then_inc(squared, 1)
                        act.wait_ge(squared, 2 * t + s + 1)
                nc.scalar.activation(nr[:, h, 0, :], ss[:, h, 0, :], ACT.Sqrt).then_inc(norms_ready, 1)
                for k in range(2):
                    nc.scalar.activation(nr[:, h, 1, k:k + 1], ss[:, h, 1, k:k + 1], ACT.Sqrt,
                                         bias=ss[:, h, 0, k:k + 1]).then_inc(norms_ready, 1)

            def o_squares(q, h):
                act.wait_ge(o_ready, q + 1)
                for k in range(2):
                    t = 2 * q + k
                    act.wait_ge(ss3_done, 4 + t)
                    nc.scalar.activation(junk[:, 0:OUT3].rearrange("p (g d) -> p g d", d=HD), raw[:, h, k, 2, :, :],
                                         ACT.Square, accum_out=ss3[:, ds(t, 1)]).then_inc(ss3_done, 1)

            def copy_oT(q):
                for k in range(2):
                    t = 2 * q + k
                    act.wait_ge(oT_ready, 4 + t + 1)
                    act.wait_ge(ft_ready, t + 1)
                    nc.scalar.activation(oT[:, k, :, :], oT_ps[:, :, :], ACT.Copy).then_inc(oT_kept, 1)

            def chunk(i):
                for h in range(2):
                    q = 2 * i + h
                    if valid(q, PAIRS):
                        keep(q, h)
                    if valid(q - 1, PAIRS):
                        copy_oT(q - 1)
                        o_squares(q - 1, 1 - h)
            act.sem_inc(norms_ready, 1)
            pipelined(act, chunk, CHUNKS)

        SMALL = 21

        @block.vector
        def _(dve):
            dve.sem_inc(ft_kept, 1)
            first = Order(dve, small)
            first.then(nc.vector.memset(w_bd[:, :, :], 0.0))
            dve.wait_ge(w_in, 96)
            for c in range(CT):
                first.then(nc.vector.tensor_scalar(w_bd[:, c, :], w_bd[:, c, :], w_dw[:, c:c + 1], None, ALU.mult))

            def attend(q, h):
                od = Order(dve, small, 1 + CT + q * SMALL)
                then = od.then
                rq, rk, rv = (raw[:, h, :, n, :, :].rearrange("p t g d -> p t (g d)") for n in range(3))
                rk3 = raw[:, h, :, 1, :, :]
                dve.wait_ge(us_kept, 2 + 2 * q + 2)
                dve.wait_ge(squared, 4 * q + 4)
                then(nc.vector.tensor_scalar(rk, rk, 0.0, None, ALU.max))
                then(nc.vector.tensor_reduce(ksum[:, :, :], rk3, X, ALU.add))
                dve.wait_ge(norms_ready, 1 + 3 * q + 3)
                then(nc.vector.tensor_scalar(f["a"][:, :], nr[:, h, 0, :], MIN_NORM, None, ALU.max))
                then(nc.vector.reciprocal(f["a"][:, :], f["a"][:, :]))
                then(nc.vector.scalar_tensor_tensor(f["c1"][:, :], nr[:, h, 0, :], RADIUS, f["a"][:, :], ALU.min, ALU.mult))
                then(nc.vector.tensor_tensor(f["n2"][:, :], nr[:, h, 1, :], f["c1"][:, :], ALU.mult))
                then(nc.vector.tensor_scalar(f["a"][:, :], f["n2"][:, :], MIN_NORM, None, ALU.max))
                then(nc.vector.reciprocal(f["a"][:, :], f["a"][:, :]))
                then(nc.vector.scalar_tensor_tensor(f["b"][:, :], f["n2"][:, :], RADIUS, f["a"][:, :], ALU.min, ALU.mult))
                then(nc.vector.tensor_tensor(f["c"][:, :], f["c1"][:, :], f["b"][:, :], ALU.mult))
                then(nc.vector.tensor_tensor(f["cc"][:, :], f["c"][:, :], f["c"][:, :], ALU.mult))
                for k in range(2):
                    then(nc.vector.tensor_scalar(ksum[:, k, :], ksum[:, k, :], f["cc"][:, k:k + 1], None, ALU.mult))
                    then(nc.vector.tensor_scalar(raw[:, h, k, 2, :, :], raw[:, h, k, 2, :, :], f["c"][:, k:k + 1], None, ALU.mult))
                for k in range(2):
                    then(nc.vector.scalar_tensor_tensor(
                        raw[:, h, k, 0, :, :], raw[:, h, k, 0, :, :], 0.0, ksum[:, k, :].unsqueeze(2).broadcast_to([P, HEADS, HD]),
                        ALU.max, ALU.mult))
                then(nc.vector.tensor_scalar(rk, rv, MIN_NORM, None, ALU.add))
                then(nc.vector.reciprocal(rk, rk))
                then(nc.vector.tensor_tensor(rk, rk, rq, ALU.mult))
                then(nc.vector.tensor_tensor(rv, rv, rk, ALU.mult))
                dve.sem_inc(o_ready, 1)
                assert od.n == SMALL, od.n

            def keep_ft(q):
                dve.wait_ge(ft_ready, 2 + 2 * q + 2)
                nc.vector.tensor_copy(uT[:, 0:KD, ds(2 * q * P, 2 * P)].rearrange("p k (t d) -> p k t d", t=2),
                                      ft_ps[:, :, :].rearrange("p t (k d) -> p k t d", k=KD)).then_inc(ft_kept, 1)

            def chunk(i):
                for h in range(2):
                    q = 2 * i + h
                    if valid(q - 2, PAIRS):
                        keep_ft(q - 2)
                    if valid(q, PAIRS):
                        attend(q, h)
            pipelined(dve, chunk, CHUNKS)


def mixer_out(nc, sems, w, uT, ss3, x_rows, x_mix):
    x_in = sems(*(f"x_in6_{j}" for j in range(CH)))
    b_in, v, s_act, ft_done, ft_sq, sum_done, out_done, sum_stored = sems(
        "b_in6", "s6_vector", "s6_scalar", "ft_done", "ft_sq", "sum_done", "out_done6", "sum_stored")
    with ExitStack() as ctx:
        sb, ps = allocators(nc, ctx)
        xb = sb("xb6", [P, CH, D])
        xo = sb("xo6", [P, 2, D])
        b_res = sb("b_res", [P, D])
        junk = sb("junk6", [P, D])
        n3, c3, ss4, n4, c4, th = (sb(f"f6_{k}", [P, TILES]) for k in range(6))
        block = ctx.enter_context(nc.Block())

        @block.sync
        def _(sp):
            sp.dma_start(b_res[:, :], w["b_res"].partition_broadcast(P)).then_inc(b_in, 16)
            with sp.Fori(0, CHUNKS) as i:
                for j in range(CH):
                    sp.wait_ge(sum_done, i * CH + j + 1)
                    sp.dma_start(xb[:, j, :], x_rows[:, ds(i * CH + j, 1), :]).then_inc(x_in[j], 16)

        @block.scalar
        def _(act):
            nc.scalar.activation(n3[:, :], ss3[:, :], ACT.Sqrt).then_inc(s_act, 1)
            with act.Fori(0, TILES) as t:
                act.wait_ge(ft_done, t + 1)
                act.wait_ge(ft_sq, t + 1)
                nc.scalar.activation(junk[:, :].rearrange("p (k d) -> p k d", k=KD), uT[:, 0:KD, ds(t * P, P)], ACT.Square,
                                     accum_out=ss4[:, ds(t, 1)]).then_inc(ft_sq, 1)
            act.wait_ge(ft_sq, 1 + TILES)
            nc.scalar.activation(n4[:, :], ss4[:, :], ACT.Sqrt).then_inc(s_act, 1)
            act.wait_ge(s_act, 2)
            nc.scalar.activation(th[:, :], n4[:, :], ACT.Tanh).then_inc(s_act, 1)

        @block.vector
        def _(dve):
            dve.sem_inc(sum_done, CH)
            dve.sem_inc(ft_sq, 1)
            then = Order(dve, v).then
            dve.wait_ge(s_act, 1)
            then(nc.vector.tensor_scalar(c3[:, :], n3[:, :], MIN_NORM, None, ALU.max))
            then(nc.vector.reciprocal(c3[:, :], c3[:, :]))
            then(nc.vector.scalar_tensor_tensor(c3[:, :], n3[:, :], RADIUS, c3[:, :], ALU.min, ALU.mult))
            dve.wait_ge(b_in, 16)
            with dve.Fori(0, TILES) as t:
                at = uT[:, 0:KD, ds(t * P, P)]
                nc.vector.scalar_tensor_tensor(at, at, c3[:, ds(t, 1)], b_res[:, :].rearrange("p (k d) -> p k d", k=KD),
                                               ALU.mult, ALU.add).then_inc(ft_done, 1)
            dve.wait_ge(s_act, 3)
            then(nc.vector.tensor_scalar(c4[:, :], n4[:, :], MIN_NORM, None, ALU.max))
            then(nc.vector.reciprocal(c4[:, :], c4[:, :]))
            then(nc.vector.scalar_tensor_tensor(c4[:, :], th[:, :], MAX_NORM, c4[:, :], ALU.min, ALU.mult))
            with dve.Fori(0, CHUNKS) as i:
                for j in range(CH):
                    t = i * CH + j
                    dve.wait_ge(x_in[j], 16 * i + 16)
                    dve.wait_ge(sum_stored, t + 1)
                    nc.vector.scalar_tensor_tensor(
                        xo[:, j % 2, :].rearrange("p (k d) -> p k d", k=KD), uT[:, 0:KD, ds(t * P, P)], c4[:, ds(t, 1)],
                        xb[:, j, :].rearrange("p (k d) -> p k d", k=KD), ALU.mult, ALU.add).then_inc(sum_done, 1)

        @block.gpsimd
        def _(pool):
            pool.sem_inc(sum_stored, 2)
            with pool.Fori(0, CHUNKS) as i:
                for j in range(CH):
                    t = i * CH + j
                    pool.wait_ge(sum_done, CH + t + 1)
                    pool.dma_start(x_mix[:, ds(t, 1), :], xo[:, j % 2, :]).then_inc(out_done, 16)
                    pool.wait_ge(out_done, 16 * t + 16)
                    pool.sem_inc(sum_stored, 1)


RING_GROUPS = -(-GROUPS // RING) * RING
REAL_WINDOWS = WINDOWS + 1
TAB_RING = 4
SCORE_W = D + 1


def step_table(nc, sems, dst_rows, lists, table, cum_row):
    loaded, chain, shared_out, shared_in, col_ready, col_stored, col_out, iota_done = sems(
        "loaded7", "chain7", "shared_out", "shared_in", "col_ready", "col_stored", "col_out", "iota7_done")
    with ExitStack() as ctx:
        sb, ps = allocators(nc, ctx)
        d_in = sb("d_in", [P, 4, GE], I32)
        low = sb("low", [P, 4], I32)
        high = sb("high", [P, 4], I32)
        real = sb("real7", [P, 4])
        own = sb("own", [P, 2, 4])
        allg = sb("allg", [P, 2, 4 * P])
        cum, before, f, df, zero, junk = (sb(f"t7_{n}", [P, 4 * P]) for n in range(6))
        iota = sb("iota7", [P, 1], I32)
        sv = sb("sv", [P, 1])
        gw = sb("gw", [P, 2])
        gw_i = sb("gw_i", [P, 2, 2], I32)
        cum_i = sb("cum_i", [P, 4 * P], I32)
        block = ctx.enter_context(nc.Block())

        @block.gpsimd
        def _(pool):
            nc.gpsimd.iota(iota[:, :], pattern=[[0, 1]], base=0, channel_multiplier=1).then_inc(iota_done, 1)

        @block.sync
        def _(sp):
            sp.dma_start(d_in[:, :, :], dst_rows).then_inc(loaded, 16)
            sp.wait_ge(chain, 10)
            for n in range(2):
                sp.dma_start(lists[n, :].rearrange("(p c) -> p c", c=4), own[:, n, :]).then_inc(shared_out, 16)
            sp.wait_ge(shared_out, 32)
            for n in range(2):
                sp.dma_start(allg[:, n, :], lists[n, :].partition_broadcast(P)).then_inc(shared_in, 16)
            sp.wait_ge(chain, 17)
            steps = sp.value_load(cum_i[0:1, GROUPS - 1:GROUPS], min_val=GROUPS, max_val=GROUPS * WINDOWS)
            sp.dma_start(cum_row[0:1, :], cum_i[0:1, 0:RING_GROUPS]).then_inc(shared_in, 16)
            with sp.Fori(0, (steps + 3 + P - 1) >> 7) as c:
                row = sp.snap(c * P)
                sp.wait_ge(col_ready, c + 1)
                sp.dma_start(table[ds(row, P), :], gw_i[:, 0, :]).then_inc(col_out, 16)
                sp.wait_ge(col_out, 16 * c + 16)
                sp.sem_inc(col_stored, 1)
            sp.wait_ge(shared_in, 48)

        @block.vector
        def _(dve):
            then = Order(dve, chain).then
            dve.wait_ge(loaded, 16)
            then(nc.vector.tensor_reduce(low[:, :], d_in[:, :, :], X, ALU.min))
            then(nc.vector.tensor_reduce(high[:, :], d_in[:, :, :], X, ALU.max))
            then(nc.vector.tensor_scalar(real[:, :], low[:, :], float(NODES), None, ALU.is_lt))
            then(nc.vector.tensor_scalar(high[:, :], high[:, :], float(NODES - 1), None, ALU.min))
            then(nc.vector.tensor_scalar(low[:, :], low[:, :], 7, None, ALU.arith_shift_right))
            then(nc.vector.tensor_scalar(high[:, :], high[:, :], 7, None, ALU.arith_shift_right))
            then(nc.vector.tensor_tensor(own[:, 0, :], high[:, :], low[:, :], ALU.subtract))
            then(nc.vector.tensor_scalar(own[:, 0, :], own[:, 0, :], 1.0, None, ALU.add))
            then(nc.vector.tensor_tensor(own[:, 0, :], own[:, 0, :], real[:, :], ALU.mult))
            then(nc.vector.tensor_copy(own[:, 1, :], low[:, :]))
            then(nc.vector.memset(zero[:, :], 0.0))
            dve.wait_ge(shared_in, 32)
            then(nc.vector.tensor_tensor_scan(cum[:, :], allg[:, 0, :], zero[:, :], 0.0, ALU.add, ALU.add))
            then(nc.vector.tensor_tensor(before[:, :], cum[:, :], allg[:, 0, :], ALU.subtract))
            then(nc.vector.tensor_tensor(f[:, :], allg[:, 1, :], before[:, :], ALU.subtract))
            then(nc.vector.tensor_copy(df[:, 0:1], f[:, 0:1]))
            then(nc.vector.tensor_copy(cum_i[:, :], cum[:, :]))
            then(nc.vector.tensor_scalar(cum_i[:, GROUPS:GROUPS + 1], cum[:, GROUPS:GROUPS + 1], -1.0, None, ALU.add))
            then(nc.vector.tensor_tensor(df[:, 1:4 * P], f[:, 1:4 * P], f[:, 0:4 * P - 1], ALU.subtract))
            dve.wait_ge(iota_done, 1)
            then(nc.vector.tensor_copy(sv[:, :], iota[:, :]))
            dve.sem_inc(col_stored, 1)
            steps = dve.value_load(cum_i[0:1, GROUPS - 1:GROUPS], min_val=GROUPS, max_val=GROUPS * WINDOWS)
            with dve.Fori(0, (steps + 3 + P - 1) >> 7) as c:
                in_loop = Order(dve, chain, c * 6 + 19)
                in_loop.then(nc.vector.tensor_scalar(junk[:, :], before[:, :], sv[:, :], 0.0, ALU.is_le, ALU.add,
                                                     accum_out=gw[:, 0:1]))
                in_loop.then(nc.vector.scalar_tensor_tensor(junk[:, :], before[:, :], sv[:, :], df[:, :], ALU.is_le, ALU.mult,
                                                            accum_out=gw[:, 1:2]))
                in_loop.then(nc.vector.tensor_tensor(gw[:, 1:2], gw[:, 1:2], sv[:, :], ALU.add))
                dve.wait_ge(col_stored, c + 1)
                in_loop.then(nc.vector.tensor_scalar(gw_i[:, 0, 0:1], gw[:, 0:1], -1.0, float(GROUPS - 1), ALU.add, ALU.min))
                in_loop.then(nc.vector.tensor_scalar(sv[:, :], sv[:, :], float(P), None, ALU.add))
                in_loop.then(nc.vector.tensor_scalar(gw_i[:, 0, 1:2], gw[:, 1:2], float(WINDOWS), None, ALU.min))
                dve.sem_inc(col_ready, 1)


def attention(nc, sems, w, ident, el_tab, er_rows, table, cum_row, acc, negm_all):
    names = ("in8", "idx_ready", "groups_ready", "tab_out", "steps_ready", "pen_ready", "stp_ready", "st_ready", "me_ready",
             "z_read", "zp_ready", "b_chain", "scored", "masked", "mt_ready", "max_read", "c_chain", "p_ready", "seg_ready",
             "acc_done", "setup8", "conv8", "me_kept")
    (in8, idx_ready, groups_ready, tab_out, steps_ready, pen_ready, stp_ready, st_ready, me_ready, z_read, zp_ready, b_chain,
     scored, masked, mt_ready, max_read, c_chain, p_ready, seg_ready, acc_done, setup, conv, me_kept) = sems(*names)
    gathered = sems(*(f"gathered_{r}" for r in range(RING)))
    with ExitStack() as ctx:
        sb, ps = allocators(nc, ctx)
        er = sb("er", [P, TILES, ROW_T])
        iota = sb("iota8", [P, REAL_WINDOWS * P])
        el = sb("el", [P, RING, CH, ROW_T])
        src = sb("src", [P, RING_GROUPS * CH], I32)
        dst = sb("dst", [P, RING_GROUPS * CH])
        idx = sb("idx", [P, RING, CH], I32)
        tab = sb("tab", [1, TAB_RING * CH * 2], I32)
        z = sb("z", [P, CH, SCORE_W])
        junk = sb("junk8", [P, D])
        attn_b = sb("attn_b8", [P, D])
        ones = sb("ones8", [P, 1])
        pen = sb("pen", [P, 4, CH, P])
        st = sb("st", [P, 4, CH, P])
        relu_part = sb("relu_part", [P, CH])
        score = sb("score", [P, 4, CH])
        mx = sb("mx", [P, 1])
        negm = sb("negm", [P, 4])
        drop = sb("drop", [P, 4])
        edge_m = sb("edge_m", [P, 4, CH])
        keep = sb("keep", [P, 4])
        st_ps = ps("st_ps", [P, CH, P])
        z_ps = ps("z_ps", [P, CH, 512])
        me_ps = ps("me_ps", [P, 512])
        mt_ps = ps("mt_ps", [P, CH, P])
        seg_ps = ps("seg_ps", [P, 512])
        block = ctx.enter_context(nc.Block())

        def steps_of(eng):
            last_step = eng.value_load(cum_row[0:1, GROUPS:GROUPS + 1], min_val=GROUPS - 1, max_val=GROUPS * WINDOWS - 1)
            return (last_step >> 2) + 1

        def entry(eng, i, h, what, top):
            at = ((i * CH + h) & (TAB_RING * CH - 1)) * 2 + what
            return eng.value_load(tab[0:1, ds(at, 1)], min_val=0, max_val=top)

        def group(eng, i, h):
            return entry(eng, i, h, 0, GROUPS - 1)

        def window(eng, i, h):
            return entry(eng, i, h, 1, WINDOWS)

        def run(eng, sections):
            chunks = steps_of(eng)

            def chunk(i, has):
                if has != "last":
                    eng.wait_ge(steps_ready, i + 1)
                for h in range(CH):
                    for lag, section in sections:
                        if has == "all" or (h >= lag if has == "first" else h < lag):
                            section(i, h - lag, (h - lag) % 4)
            chunk(0, "first")
            with eng.Fori(1, chunks) as i:
                chunk(i, "all")
            chunk(chunks, "last")

        @block.sync
        def _(sp):
            for quarter in range(4):
                at = slice(quarter * TILES // 4, (quarter + 1) * TILES // 4)
                sp.dma_start(er[:, at, :], er_rows[:, at, :]).then_inc(in8, 16)
            sp.dma_start(attn_b[:, :], w["attn"].partition_broadcast(P)).then_inc(in8, 16)
            chunks = steps_of(sp)
            with sp.Fori(0, chunks) as i:
                wait_apart(sp, acc_done, i * CH + CH, (in8, 80))
                sp.dma_start(tab[0:1, ds((i & (TAB_RING - 1)) * (CH * 2), CH * 2)],
                             table[ds(i * CH, CH), :].rearrange("(a s) n -> a (s n)", a=1)).then_inc(tab_out, 16)
                sp.wait_ge(tab_out, i * 16 + 16)
                sp.sem_inc(steps_ready, 1)

        @block.gpsimd
        def _(pool):
            pool.dma_start(src[:, :], w["src"]).then_inc(conv, 16)
            pool.dma_start(dst[:, :], w["dst"]).then_inc(conv, 16)
            nc.gpsimd.iota(iota[:, :], pattern=[[1, REAL_WINDOWS * P]], base=0, channel_multiplier=0,
                           allow_small_or_imprecise_dtypes=True).then_inc(setup, 1)
            pool.wait_ge(conv, 32)

            def gather(g, r):
                nc.gpsimd.tensor_copy(idx[:, r, :], src[:, ds(g * CH, CH)]).then_inc(idx_ready, 1)
                wait_apart(pool, idx_ready, g + 1, (conv, 32))
                for k in range(CH):
                    pool.indirect_dma_start(out=el[:, r, k, :], out_offset=None, in_=el_tab,
                                            in_offset=bass.IndirectOffsetOnAxis(ap=idx[:, r, k:k + 1], axis=0)).then_inc(gathered[r], 16)

            def arrived(turn, r):
                pool.wait_ge(gathered[r], turn * 64 + 64)
                pool.sem_inc(groups_ready, 1)

            for r in range(RING):
                gather(r, r)
                if r:
                    arrived(0, r - 1)
            with pool.Fori(1, RING_GROUPS // RING) as i:
                for r in range(RING):
                    g = i * RING + r
                    done = pool.value_load(cum_row[0:1, ds(g - RING, 1)], min_val=1, max_val=GROUPS * WINDOWS)
                    pool.wait_ge(seg_ready, done + 4)
                    gather(g, r)
                    arrived(i - 1 if r == 0 else i, (r - 1) % RING)
            arrived(RING_GROUPS // RING - 1, RING - 1)

        @block.tensor
        def _(pe):
            pe.sem_inc(me_ready, 4)
            pe.sem_inc(seg_ready, 4)
            pe.wait_ge(in8, 80)

            def transpose_pen(i, h, k4):
                s = i * CH + h
                pe.wait_ge(pen_ready, s + 1)
                pe.wait_ge(st_ready, s + 1)
                for k in range(CH):
                    last = nc.tensor.transpose(st_ps[:, k, :], pen[:, k4, k, :], ident)
                last.then_inc(stp_ready, 1)

            def spread_max(i, h, k4):
                s = i * CH + h
                pe.wait_ge(c_chain, s * 3 + 1)
                pe.wait_ge(me_kept, s + 1)
                for k in range(CH):
                    last = nc.tensor.matmul(me_ps[:, k:k + 1], st[:, k4, k, :], negm[:, k4:k4 + 1], start=True, stop=True)
                last.then_inc(me_ready, 1)

            def spread_er(i, h, k4):
                s = i * CH + h
                win = window(pe, i, h)
                pe.wait_ge(st_ready, 1 + s + 1)
                pe.wait_ge(z_read, s + 1)
                for k in range(CH):
                    last = nc.tensor.matmul(z_ps[:, k, 0:SCORE_W], st[:, k4, k, :],
                                            er[:, ds(win, 1), 0:SCORE_W].rearrange("p a n -> p (a n)"), start=True, stop=True)
                last.then_inc(zp_ready, 1)

            def transpose_masked(i, h, k4):
                s = i * CH + h
                pe.wait_ge(masked, s + 1)
                pe.wait_ge(max_read, s + 1)
                for k in range(CH):
                    last = nc.tensor.transpose(mt_ps[:, k, :], pen[:, k4, k, :], ident)
                last.then_inc(mt_ready, 1)

            def segment_sums(i, h, k4):
                s = i * CH + h
                slot = group(pe, i, h) & (RING - 1)
                pe.wait_ge(p_ready, s + 1)
                pe.wait_ge(acc_done, TAB_RING * CH + s)
                for k in range(CH):
                    last = nc.tensor.matmul(seg_ps[:, 0:ROW_T], pen[:, k4, k, :],
                                            el[:, ds(slot, 1), k, :].rearrange("p a n -> p (a n)"), start=(k == 0), stop=(k == CH - 1))
                last.then_inc(seg_ready, 1)

            run(pe, ((0, transpose_pen), (2, spread_max), (0, spread_er), (1, transpose_masked), (2, segment_sums)))

        @block.scalar
        def _(act):
            act.sem_inc(st_ready, 1)
            act.sem_inc(me_kept, 1)
            act.wait_ge(setup, 2)

            def copy_st(i, h, k4):
                s = i * CH + h
                act.wait_ge(stp_ready, s + 1)
                act.wait_ge(me_ready, s + 1)
                nc.scalar.activation(st[:, k4, :, :], st_ps[:, :, :], ACT.Identity, bias=ones[:, :], scale=1.0 / BIG).then_inc(st_ready, 1)

            def add_score(i, h, k4):
                s = i * CH + h
                act.wait_ge(scored, s + 1)
                act.wait_ge(stp_ready, s + 1)
                for k in range(CH):
                    last = nc.scalar.activation(pen[:, k4, k, :], pen[:, k4, k, :], ACT.Identity, bias=score[:, k4, k:k + 1])
                last.then_inc(masked, 1)

            def exps(i, h, k4):
                s = i * CH + h
                act.wait_ge(c_chain, s * 3 + 2)
                nc.scalar.activation(keep[:, k4:k4 + 1], drop[:, k4:k4 + 1], ACT.Exp)
                act.wait_ge(me_ready, 4 + s + 1)
                nc.scalar.activation(edge_m[:, k4, :], me_ps[:, 0:CH], ACT.Copy).then_inc(me_kept, 1)
                act.wait_ge(me_kept, 1 + s + 1)
                for k in range(CH):
                    last = nc.scalar.activation(pen[:, k4, k, :], pen[:, k4, k, :], ACT.Exp, bias=edge_m[:, k4, k:k + 1])
                last.then_inc(p_ready, 1)

            run(act, ((0, copy_st), (2, exps), (1, add_score)))

        @block.vector
        def _(dve):
            dve.sem_inc(z_read, 1)
            dve.sem_inc(max_read, 1)
            dve.sem_inc(acc_done, TAB_RING * CH)
            nc.vector.memset(ones[:, :], 1.0)
            nc.vector.memset(acc[:, :, :], 0.0)
            nc.vector.memset(negm_all[:, :], BIG).then_inc(setup, 1)
            dve.wait_ge(in8, 80)
            nc.vector.tensor_scalar(attn_b[:, :], attn_b[:, :], 1.0 - SLOPE, None, ALU.mult).then_inc(b_chain, 1)
            dve.wait_ge(b_chain, 1)
            dve.wait_ge(setup, 2)
            dve.wait_ge(conv, 32)

            def mask(i, h, k4):
                s = i * CH + h
                g, win = group(dve, i, h), window(dve, i, h)
                dve.wait_ge(seg_ready, s + 1)
                for k in range(CH):
                    last = nc.vector.tensor_scalar(pen[:, k4, k, :], iota[:, ds(win * P, P)], dst[:, ds(g * CH + k, 1)], -BIG,
                                                   ALU.not_equal, ALU.mult)
                last.then_inc(pen_ready, 1)

            def maxima(i, h, k4):
                s = i * CH + h
                win = window(dve, i, h)
                dve.wait_ge(mt_ready, s + 1)
                nc.vector.tensor_reduce(mx[:, :], mt_ps[:, :, :].rearrange("p k n -> p (k n)"), X, ALU.max).then_inc(max_read, 1)
                dve.wait_ge(max_read, 1 + s + 1)
                dve.wait_ge(c_chain, s * 3)
                c = Order(dve, c_chain, s * 3)
                c.then(nc.vector.scalar_tensor_tensor(negm[:, k4:k4 + 1], mx[:, :], -1.0, negm_all[:, ds(win, 1)], ALU.mult, ALU.min))
                c.then(nc.vector.tensor_tensor(drop[:, k4:k4 + 1], negm[:, k4:k4 + 1], negm_all[:, ds(win, 1)], ALU.subtract))
                nc.vector.tensor_scalar(negm_all[:, ds(win, 1)], negm[:, k4:k4 + 1], 0.0, None, ALU.add).then_inc(c_chain, 1)

            def scores(i, h, k4):
                s = i * CH + h
                g = group(dve, i, h)
                dve.wait_ge(zp_ready, s + 1)
                dve.wait_ge(groups_ready, g + 1)
                nc.vector.tensor_tensor(z[:, :, :], z_ps[:, :, 0:SCORE_W],
                                        el[:, ds(g & (RING - 1), 1), :, 0:SCORE_W].rearrange("p a k n -> p (a k) n"), ALU.add).then_inc(z_read, 1)
                dve.wait_ge(z_read, 1 + s + 1)
                b = Order(dve, b_chain, 1 + s * CH)
                for k in range(CH):
                    b.then(nc.vector.scalar_tensor_tensor(junk[:, :], z[:, k, 0:D], 0.0, attn_b[:, :], ALU.max, ALU.mult,
                                                          accum_out=relu_part[:, k:k + 1]))
                nc.vector.tensor_tensor(score[:, k4, :], relu_part[:, :], z[:, :, D], ALU.add).then_inc(scored, 1)

            def accumulate(i, h, k4):
                s = i * CH + h
                win = window(dve, i, h)
                dve.wait_ge(seg_ready, 4 + s + 1)
                at = acc[:, ds(win, 1), :].rearrange("p a n -> p (a n)")
                dve.wait_ge(acc_done, TAB_RING * CH + s)
                nc.vector.scalar_tensor_tensor(at, at, keep[:, k4:k4 + 1], seg_ps[:, 0:ROW_T], ALU.mult, ALU.add).then_inc(acc_done, 1)

            run(dve, ((0, mask), (3, accumulate), (2, maxima), (1, scores)))


OUT_ROWS = WINDOWS * P
G7 = 7
assert WINDOWS % G7 == 0


def residual_sum(nc, sems, x_mix, acc, st, zeros, moe_in):
    z_chain, x2_done, stats_done, zero_out = sems("z_chain", "x2_done", "stats_done9", "zero_out")
    x_in = sems(*(f"x_in9_{j}" for j in range(G7)))
    with ExitStack() as ctx:
        sb, ps = allocators(nc, ctx)
        xb = sb("xb9", [P, G7, D])
        rz = sb("rz", [P, WINDOWS])
        block = ctx.enter_context(nc.Block())

        @block.sync
        def _(sp):
            with sp.Fori(0, WINDOWS // G7) as i:
                for j in range(G7):
                    sp.wait_ge(x2_done, i * G7 + j + 1)
                    sp.dma_start(xb[:, j, :], x_mix[:, ds(i * G7 + j, 1), :]).then_inc(x_in[j], 16)

        @block.scalar
        def _(act):
            act.wait_ge(z_chain, 1)
            act.dma_start(moe_in.rearrange("(n p) d -> p n d", p=TT),
                          zeros[0:TT, :].unsqueeze(1).broadcast_to([TT, EXPERTS * ET, D])).then_inc(zero_out, 16)
            act.wait_ge(zero_out, 16)

        @block.vector
        def _(dve):
            dve.sem_inc(x2_done, G7)
            then = Order(dve, z_chain).then
            then(nc.vector.memset(zeros[:, :], 0.0))
            then(nc.vector.tensor_scalar(rz[:, :], acc[:, 0:WINDOWS, D + 1], 1e-30, None, ALU.max))
            then(nc.vector.reciprocal(rz[:, :], rz[:, :]))
            with dve.Fori(0, WINDOWS // G7) as i:
                for j in range(G7):
                    t = i * G7 + j
                    dve.wait_ge(x_in[j], 16 * i + 16)
                    at = acc[:, ds(t, 1), 0:D].rearrange("p a d -> p (a d)")
                    nc.vector.scalar_tensor_tensor(at, at, rz[:, ds(t, 1)], xb[:, j, :], ALU.mult, ALU.add).then_inc(x2_done, 1)
                    dve.wait_ge(x2_done, G7 + t + 1)
                    nc.vector.bn_stats(st[:, ds(t, 1), :], at)


def route(nc, sems, w, ident, x2, st, a, r, moe_in):
    names = ("in10", "consts", "m_chain", "m_act", "y_ready", "yT_ready", "yT_kept", "logit_ready", "logit_kept", "r_chain",
             "r_act", "counts", "slot_ready", "y2_ready", "scattered", "slot_free")
    (in10, consts, m_chain, m_act, y_ready, yT_ready, yT_kept, logit_ready, logit_kept, r_chain, r_act, counts, slot_ready,
     y2_ready, scattered, slot_free) = sems(*names)
    E, N = EXPERTS, WINDOWS
    ONEHOT = 10
    with ExitStack() as ctx:
        sb, ps = allocators(nc, ctx)
        gate_w = sb("gate_w", [P, KD, E])
        gate_b = sb("gate_b", [P, E])
        y = sb("y10", [P, D])
        yT = sb("yT", [P, KD, P])
        tri = sb("tri", [P, P])
        ones = sb("ones10", [P, P])
        token = sb("token", [P, N], I32)
        rank = sb("rank", [P, E], I32)
        logits, key, oh, base, ex = (sb(f"r_{n}", [P, E, N]) for n in ("logits", "key", "oh", "base", "ex"))
        rk = sb("rk", [P, E])
        mx, km, pos, real, kept, t0, slot_s, slot_g = (sb(f"r10_{n}", [P, N]) for n in range(8))
        slot_i = sb("slot_i", [P, N], I32)
        idx = sb("idx10", [P, 2, 1], I32)
        y2 = sb("y2", [P, 2, D])
        yT_ps = ps("yT_ps", [P, KD, P])
        lg_ps = ps("lg_ps", [P, 512])
        cnt_ps = ps("cnt_ps", [P, E * N])
        tot_ps = ps("tot_ps", [P, E * N])
        block = ctx.enter_context(nc.Block())

        @block.sync
        def _(sp):
            sp.dma_start(gate_w[:, :, :], w["gate_w"].rearrange("(k p) e -> p k e", p=P)).then_inc(in10, 16)
            sp.dma_start(gate_b[:, :], w["gate_b"].partition_broadcast(P)).then_inc(in10, 16)

        @block.gpsimd
        def _(pool):
            nc.gpsimd.memset(ones[:, :], 1.0).then_inc(consts, 1)
            nc.gpsimd.iota(token[:, :], pattern=[[P, N]], base=0, channel_multiplier=1).then_inc(consts, 1)
            nc.gpsimd.iota(rank[:, :], pattern=[[-1, E]], base=E, channel_multiplier=0).then_inc(consts, 1)
            pool.wait_ge(consts, 3)
            nc.gpsimd.affine_select(out=tri[:, :], in_=ones[:, :], compare_op=ALU.is_ge, fill=0.0, base=0,
                                    pattern=[[1, P]], channel_multiplier=-1).then_inc(consts, 1)
            pool.sem_inc(slot_free, 2)

            def scatter(t, k):
                wait_apart(pool, slot_ready, t + 1, (consts, 4))
                pool.wait_ge(y2_ready, t + 1)
                pool.indirect_dma_start(out=moe_in, out_offset=bass.IndirectOffsetOnAxis(ap=idx[:, k, :], axis=0),
                                        in_=y2[:, k, :], in_offset=None, bounds_check=EXPERTS * SLOTS - 1,
                                        oob_is_err=False).then_inc(scattered, 16)
                pool.wait_ge(scattered, 16 * t + 16)
                pool.sem_inc(slot_free, 1)
            scatter(0, 0)
            with pool.Fori(0, N // 2) as i:
                scatter(2 * i + 1, 1)
                scatter(2 * i + 2, 0)

        @block.tensor
        def _(pe):
            pe.sem_inc(yT_ready, 1)
            pe.sem_inc(logit_ready, 1)
            pe.wait_ge(in10, 32)
            pe.wait_ge(consts, 4)
            with pe.Fori(0, N) as t:
                pe.wait_ge(y_ready, t + 1)
                pe.wait_ge(yT_kept, t + 1)
                for k in range(KD):
                    last = nc.tensor.transpose(yT_ps[:, k, :], y[:, k * P:(k + 1) * P], ident)
                last.then_inc(yT_ready, 1)
                pe.wait_ge(yT_kept, 1 + t + 1)
                pe.wait_ge(logit_kept, t + 1)
                for k in range(KD):
                    last = nc.tensor.matmul(lg_ps[:, 0:E], yT[:, k, :], gate_w[:, k, :], start=(k == 0), stop=(k == KD - 1))
                last.then_inc(logit_ready, 1)
            pe.wait_ge(r_chain, ONEHOT)
            nc.tensor.matmul(cnt_ps[:, :], tri[:, :], oh[:, :, :].rearrange("p e n -> p (e n)"), start=True, stop=True)
            nc.tensor.matmul(tot_ps[:, :], ones[:, :], oh[:, :, :].rearrange("p e n -> p (e n)"), start=True, stop=True).then_inc(counts, 1)

        @block.scalar
        def _(act):
            act.sem_inc(yT_kept, 1)
            act.wait_ge(m_chain, MOMENT_OPS)
            nc.scalar.activation(a["sd"][:, 0:N], a["var_e"][:, 0:N], ACT.Sqrt).then_inc(m_act, 1)
            with act.Fori(0, N) as t:
                act.wait_ge(yT_ready, 1 + t + 1)
                act.wait_ge(logit_ready, t + 1)
                nc.scalar.activation(yT[:, :, :], yT_ps[:, :, :], ACT.Copy).then_inc(yT_kept, 1)
            act.wait_ge(r_chain, 2)
            nc.scalar.activation(ex[:, :, :], ex[:, :, :], ACT.Exp).then_inc(r_act, 1)

        @block.vector
        def _(dve):
            row_moments(nc, dve, m_chain, st, a, N)
            dve.wait_ge(m_act, 1)
            then = Order(dve, m_chain, MOMENT_OPS).then
            then(nc.vector.reciprocal(a["rstd"][:, 0:N], a["sd"][:, 0:N]))
            dve.sem_inc(logit_kept, 1)
            dve.wait_ge(in10, 32)

            def normalise(out, t):
                return nc.vector.tensor_scalar(out, x2[:, ds(t, 1), 0:D].rearrange("p a d -> p (a d)"), a["mean"][:, ds(t, 1)],
                                               a["rstd"][:, ds(t, 1)], ALU.subtract, ALU.mult)

            with dve.Fori(0, N) as t:
                dve.wait_ge(yT_ready, t + 1)
                normalise(y[:, :], t).then_inc(y_ready, 1)
                dve.wait_ge(logit_ready, 1 + t + 1)
                nc.vector.tensor_tensor(logits[:, :, ds(t, 1)].rearrange("p e a -> p (e a)"), lg_ps[:, 0:E], gate_b[:, :],
                                        ALU.add).then_inc(logit_kept, 1)
            dve.wait_ge(logit_kept, 1 + N)
            dve.wait_ge(consts, 4)
            o = Order(dve, r_chain)
            then = o.then
            by_expert = lambda v: v[:, :, :].rearrange("p e n -> p n e")
            spread = lambda v: v[:, :].unsqueeze(1).broadcast_to([P, E, N])
            then(nc.vector.tensor_reduce(mx[:, :], by_expert(logits), X, ALU.max))
            then(nc.vector.tensor_tensor(ex[:, :, :], logits[:, :, :], spread(mx), ALU.subtract))
            then(nc.vector.tensor_copy(rk[:, :], rank[:, :]))
            then(nc.vector.tensor_scalar(real[:, :], token[:, :], float(NODES), None, ALU.is_lt))
            ranks = rk[:, :].unsqueeze(2).broadcast_to([P, E, N])
            then(nc.vector.tensor_tensor(key[:, :, :], logits[:, :, :], spread(mx), ALU.is_equal))
            then(nc.vector.tensor_tensor(key[:, :, :], key[:, :, :], ranks, ALU.mult))
            then(nc.vector.tensor_reduce(km[:, :], by_expert(key), X, ALU.max))
            then(nc.vector.tensor_copy(base[:, :, :], ranks))
            then(nc.vector.tensor_tensor(oh[:, :, :], base[:, :, :], spread(km), ALU.is_equal))
            then(nc.vector.tensor_tensor(oh[:, :, :], oh[:, :, :], spread(real), ALU.mult))
            assert o.n == ONEHOT
            dve.wait_ge(r_act, 1)
            then(nc.vector.tensor_reduce(t0[:, :], by_expert(ex), X, ALU.add))
            then(nc.vector.reciprocal(r["weight"], t0[:, :]))
            dve.wait_ge(counts, 1)
            then(nc.vector.tensor_copy(base[:, :, :].rearrange("p e n -> p (e n)"), tot_ps[:, :]))
            then(nc.vector.memset(t0[:, :], 0.0))
            for e in range(E):
                then(nc.vector.tensor_tensor_scan(key[:, e, :], base[:, e, :], t0[:, :], 0.0, ALU.add, ALU.add))
            then(nc.vector.tensor_tensor(key[:, :, :], key[:, :, :], base[:, :, :], ALU.subtract))
            then(nc.vector.tensor_tensor(key[:, :, :].rearrange("p e n -> p (e n)"), cnt_ps[:, :],
                                         key[:, :, :].rearrange("p e n -> p (e n)"), ALU.add))
            then(nc.vector.tensor_tensor(key[:, :, :], key[:, :, :], oh[:, :, :], ALU.mult))
            then(nc.vector.tensor_reduce(pos[:, :], by_expert(key), X, ALU.add))
            then(nc.vector.tensor_scalar(pos[:, :], pos[:, :], -1.0, None, ALU.add))
            then(nc.vector.tensor_scalar(kept[:, :], pos[:, :], float(CAP), None, ALU.is_lt))
            then(nc.vector.tensor_tensor(kept[:, :], kept[:, :], real[:, :], ALU.mult))
            then(nc.vector.tensor_tensor(r["weight"], r["weight"], kept[:, :], ALU.mult))
            then(nc.vector.tensor_scalar(t0[:, :], km[:, :], -float(SLOTS), float(E * SLOTS), ALU.mult, ALU.add))
            then(nc.vector.tensor_scalar(slot_g[:, :], pos[:, :], 0.0, float(CAP - 1), ALU.max, ALU.min))
            then(nc.vector.tensor_tensor(slot_g[:, :], slot_g[:, :], t0[:, :], ALU.add))
            then(nc.vector.tensor_copy(r["slot"], slot_g[:, :]))
            then(nc.vector.tensor_scalar(t0[:, :], kept[:, :], -float(NO_SLOT), float(NO_SLOT), ALU.mult, ALU.add))
            then(nc.vector.tensor_tensor(slot_s[:, :], slot_g[:, :], t0[:, :], ALU.add))
            then(nc.vector.tensor_copy(slot_i[:, :], slot_s[:, :]))

            def place(t, k):
                dve.wait_ge(slot_free, t + 1)
                normalise(y2[:, k, :], t).then_inc(y2_ready, 1)
                nc.vector.tensor_copy(idx[:, k, :], slot_i[:, ds(t, 1)]).then_inc(slot_ready, 1)
            place(0, 0)
            with dve.Fori(0, N // 2) as i:
                place(2 * i + 1, 1)
                place(2 * i + 2, 0)


def experts(nc, sems, w, ident, moe_in, moe_out):
    in11, xT_ready, xT_kept, h_ready, h_kept, y_ready, y_added, y_out, y_stored, w_used, bias_ready = sems(
        "in11", "xT_ready", "xT_kept", "hid_ready", "hid_kept", "y11_ready", "y_added", "y_out", "y_stored", "w_used", "bias_ready")
    w_in = sems("w_in11_0", "w_in11_1")
    HALF = SLOTS // 2
    with ExitStack() as ctx:
        sb, ps = allocators(nc, ctx)
        w1 = sb("w1", [P, 2, KD, FF])
        w2 = sb("w2", [P, 2, FT, D])
        xr = sb("xr", [TT, 2, ET, D])
        b1 = sb("b1", [P, EXPERTS, FT])
        b2 = sb("b2", [P, EXPERTS, D])
        b1_now = sb("b1_now", [P, FT])
        xT = sb("xT", [P, KD, SLOTS])
        hid = sb("hid", [P, FT, SLOTS])
        yr = sb("yr", [TT, 2, D])
        xT_ps = ps("xT_ps", [P, 2, KD, 256])
        h_ps = ps("hid_ps", [P, 2, 512])
        y_ps = ps("y_ps", [P, 2, 512])
        block = ctx.enter_context(nc.Block())

        @block.sync
        def _(sp):
            sp.dma_start(b1[:, :, :], w["b1"]).then_inc(in11, 16)
            sp.dma_start(b2[:, :, :].rearrange("p e d -> p (e d)"), w["b2"].rearrange("e d -> (e d)").partition_broadcast(P)).then_inc(in11, 16)
            with sp.Fori(0, EXPERTS // 2) as i:
                for k in range(2):
                    e = 2 * i + k
                    sp.wait_ge(w_used, e + 1)
                    sp.dma_start(xr[:, k, :, :], moe_in[ds(e * SLOTS, SLOTS), :].rearrange("(n p) d -> p n d", p=TT)).then_inc(w_in[k], 16)
                    sp.dma_start(w1[:, k, :, :], w["w1"][ds(e, 1), :, :].rearrange("a (k p) f -> p (a k) f", p=P)).then_inc(w_in[k], 16)
                    sp.dma_start(w2[:, k, :, :], w["w2"][ds(e, 1), :, :].rearrange("a (k p) f -> p (a k) f", p=P)).then_inc(w_in[k], 16)

        @block.tensor
        def _(pe):
            pe.sem_inc(w_used, 2)
            pe.sem_inc(y_ready, ET)
            pe.sem_inc(h_ready, 1)
            with pe.Fori(0, EXPERTS // 2) as i:
                for k in range(2):
                    e = 2 * i + k
                    pe.wait_ge(w_in[k], 48 * i + 48)
                    for n in range(ET):
                        pe.wait_ge(xT_kept, e * ET + n + 1)
                        for c in range(KD):
                            last = nc.tensor.transpose(xT_ps[:, n % 2, c, 0:TT], xr[:, k, n, c * P:(c + 1) * P], ident[0:TT, 0:TT])
                        last.then_inc(xT_ready, 1)
                    pe.wait_ge(xT_kept, 2 + e * ET + ET)
                    for f in range(FT):
                        for s in range(2):
                            n = e * FT * 2 + f * 2 + s
                            pe.wait_ge(h_kept, n + 1)
                            for c in range(KD):
                                last = nc.tensor.matmul(h_ps[:, s, 0:HALF], w1[:, k, c, f * P:(f + 1) * P],
                                                        xT[:, c, s * HALF:(s + 1) * HALF], start=(c == 0), stop=(c == KD - 1))
                            last.then_inc(h_ready, 1)
                    pe.wait_ge(h_kept, 2 + (e + 1) * FT * 2)
                    for n in range(ET):
                        pe.wait_ge(y_added, e * ET + n + 1)
                        for f in range(FT):
                            last = nc.tensor.matmul(y_ps[0:TT, n % 2, 0:D], hid[:, f, n * TT:(n + 1) * TT], w2[:, k, f, :],
                                                    start=(f == 0), stop=(f == FT - 1))
                        last.then_inc(y_ready, 1)
                    pe.wait_ge(y_ready, ET + (e + 1) * ET)
                    pe.sem_inc(w_used, 1)

        @block.scalar
        def _(act):
            act.sem_inc(h_kept, 2)
            act.wait_ge(in11, 32)
            with act.Fori(0, EXPERTS) as e:
                act.wait_ge(y_ready, e * ET + ET)
                nc.scalar.activation(b1_now[:, :], b1[:, ds(e, 1), :].rearrange("p a f -> p (a f)"), ACT.Copy).then_inc(bias_ready, 1)
                act.wait_ge(bias_ready, e + 1)
                for f in range(FT):
                    for s in range(2):
                        act.wait_ge(h_ready, 1 + e * FT * 2 + f * 2 + s + 1)
                        nc.scalar.activation(hid[:, f, s * HALF:(s + 1) * HALF], h_ps[:, s, 0:HALF], ACT.Relu,
                                             bias=b1_now[:, f:f + 1]).then_inc(h_kept, 1)

        @block.vector
        def _(dve):
            dve.sem_inc(xT_kept, 2)
            dve.sem_inc(y_added, 2)
            dve.wait_ge(in11, 32)
            with dve.Fori(0, EXPERTS) as e:
                for n in range(ET):
                    dve.wait_ge(xT_ready, e * ET + n + 1)
                    if n == 0:
                        dve.wait_ge(h_ready, e * FT * 2 + 1)
                    nc.vector.tensor_copy(xT[:, :, n * TT:(n + 1) * TT], xT_ps[:, n % 2, :, 0:TT]).then_inc(xT_kept, 1)
                for n in range(ET):
                    dve.wait_ge(y_ready, ET + e * ET + n + 1)
                    dve.wait_ge(y_stored, e * ET + n + 1)
                    nc.vector.tensor_tensor(yr[:, n % 2, :], y_ps[0:TT, n % 2, 0:D],
                                            b2[0:TT, ds(e, 1), :].rearrange("p a d -> p (a d)"), ALU.add).then_inc(y_added, 1)

        @block.gpsimd
        def _(pool):
            pool.sem_inc(y_stored, 2)
            with pool.Fori(0, EXPERTS) as e:
                for n in range(ET):
                    pool.wait_ge(y_added, 2 + e * ET + n + 1)
                    pool.dma_start(moe_out[ds(e * SLOTS + n * TT, TT), :], yr[:, n % 2, :]).then_inc(y_out, 16)
                    pool.wait_ge(y_out, 16 * (e * ET + n) + 16)
                    pool.sem_inc(y_stored, 1)


def combine(nc, sems, x2, r, zeros, moe_out, out):
    idx_ready, scaled, chain, summed, stored = sems("idx12", "scaled", "chain12", "summed", "stored12")
    got = sems(*(f"got_{j}" for j in range(G7)))
    with ExitStack() as ctx:
        sb, ps = allocators(nc, ctx)
        idx = sb("idx12_t", [P, G7, 1], I32)
        y = sb("y12", [P, G7, D])
        low, high, safe = (sb(f"t12_{n}", [P, D]) for n in range(3))
        whole = sb("whole", [P, D])
        block = ctx.enter_context(nc.Block())

        @block.gpsimd
        def _(pool):
            with pool.Fori(0, WINDOWS // G7) as i:
                for j in range(G7):
                    t = i * G7 + j
                    pool.wait_ge(summed, t + 1)
                    nc.gpsimd.tensor_copy(idx[:, j, :], r["slot"][:, ds(t, 1)]).then_inc(idx_ready, 1)
                    wait_apart(pool, idx_ready, t + 1, (summed, G7))
                    pool.indirect_dma_start(out=y[:, j, :], out_offset=None, in_=moe_out,
                                            in_offset=bass.IndirectOffsetOnAxis(ap=idx[:, j, :], axis=0)).then_inc(got[j], 16)

        @block.vector
        def _(dve):
            dve.sem_inc(summed, G7)
            with dve.Fori(0, WINDOWS // G7) as i:
                for j in range(G7):
                    t = i * G7 + j
                    o = Order(dve, chain, t * 5)
                    v = y[:, j, :]
                    dve.wait_ge(got[j], 16 * i + 16)
                    o.then(nc.vector.tensor_scalar(v, v, r["weight"][:, ds(t, 1)], None, ALU.mult))
                    nc.vector.tensor_scalar(low[:, :], v, 0.0, -10000.0, ALU.min, ALU.max)
                    nc.vector.tensor_scalar(whole[:, :], v, 0.0, 0.0, ALU.mult, ALU.is_equal)
                    o.then(nc.vector.tensor_scalar(high[:, :], v, 0.0, 10000.0, ALU.max, ALU.min))
                    nc.vector.tensor_tensor(safe[:, :], low[:, :], high[:, :], ALU.add).then_inc(chain, 1)
                    o.n += 1
                    wait_apart(dve, chain, t * 5 + o.n, (summed, G7))
                    o.then(nc.vector.copy_predicated(safe[:, :], whole[:, :].bitcast(I32), v))
                    at = x2[:, ds(t, 1), 0:D].rearrange("p a d -> p (a d)")
                    o.then(nc.vector.tensor_tensor(at, at, safe[:, :], ALU.add))
                    dve.sem_inc(summed, 1)

        @block.sync
        def _(sp):
            with sp.Fori(0, WINDOWS) as t:
                sp.wait_ge(summed, G7 + t + 1)
                sp.dma_start(out[:, ds(t, 1), :], x2[:, ds(t, 1), 0:D]).then_inc(stored, 16)
            sp.wait_ge(stored, 16 * WINDOWS)


def constants(nc, sems, ident):
    zero_done, ident_done = sems("ident_zero", "ident_done")
    with nc.Block() as block:
        @block.gpsimd
        def _(pool):
            nc.gpsimd.memset(ident, 0.0).then_inc(zero_done, 1)
            pool.wait_ge(zero_done, 1)
            nc.gpsimd.affine_select(out=ident, in_=ident, compare_op=ALU.not_equal, fill=1.0, base=0,
                                    pattern=[[-1, P]], channel_multiplier=1).then_inc(ident_done, 1)
            pool.wait_ge(ident_done, 1)


def layouts(x, src, dst, L0_gnn_W_src, L0_gnn_b_src, L0_gnn_W_dst, L0_gnn_b_dst, L0_gnn_attn, L0_mix_w_qkv,
            L0_mix_bn_gamma, L0_mix_bn_beta, L0_mix_w_dw, L0_mix_w_pw, L0_mix_w_res, L0_mix_b_res, L0_ffn_gate_w,
            L0_ffn_gate_b, L0_ffn_w1, L0_ffn_b1, L0_ffn_w2, L0_ffn_b2):
    def columns(v, n):
        return v.reshape(n, P).T

    def edges(v, fill):
        padded = np.full(RING_GROUPS * GE, fill, np.int32)
        padded[:EDGES] = v
        return padded.reshape(RING_GROUPS * CH, P).T

    def by_part(v):
        return v.reshape(8, 3, HD, *v.shape[1:]).swapaxes(0, 1).reshape(v.shape)

    rows = np.zeros((ROWS, D), np.float32)
    rows[:NODES] = x
    by_group = np.full(4 * P * GE, NO_NODE, np.int32)
    by_group[:EDGES] = dst
    return {
        "x": rows, "src": edges(src, 0), "dst": edges(dst, NO_NODE),
        "dst_rows": by_group.reshape(P, 4, GE),
        "W_src": L0_gnn_W_src, "W_dst": L0_gnn_W_dst, "b_src": L0_gnn_b_src, "b_dst": L0_gnn_b_dst, "attn": L0_gnn_attn,
        "w_qkv": by_part(L0_mix_w_qkv[:, :, 2]).T, "gamma": columns(by_part(L0_mix_bn_gamma), CT),
        "beta": columns(by_part(L0_mix_bn_beta), CT), "w_dw": columns(by_part(L0_mix_w_dw[:, 0, 2]), CT),
        "w_pw": by_part(L0_mix_w_pw[:, :, 0]).reshape(CT, 4, HD, HD).transpose(1, 3, 0, 2),
        "w_res": L0_mix_w_res[:, :, 0].T, "b_res": L0_mix_b_res,
        "gate_w": L0_ffn_gate_w, "gate_b": L0_ffn_gate_b,
        "w1": L0_ffn_w1, "w2": L0_ffn_w2, "b2": L0_ffn_b2,
        "b1": L0_ffn_b1.reshape(EXPERTS, FT, P).transpose(2, 0, 1),
    }


def kernel(**inputs):
    import concourse.bacc as _bacc
    from concourse.bass_utils import run_bass_kernel_spmd as _run
    arrays = {n: np.ascontiguousarray(a) for n, a in layouts(**{n: np.asarray(a) for n, a in inputs.items()}).items()}
    nc = _bacc.Bacc("TRN2", target_bir_lowering=False, num_devices=1)
    tensors = {n: nc.dram_tensor(f"in_{n}", a.shape, mybir.dt.from_np(a.dtype), kind="ExternalInput").ap() for n, a in arrays.items()}
    out = nc.dram_tensor("out_rows", [OUT_ROWS, D], F32, kind="ExternalOutput").ap()
    program(nc, tensors, out)
    r = _run(nc, [{f"in_{n}": a for n, a in arrays.items()}], core_ids=[0])
    return r.results[0]["out_rows"][:NODES]
```
